# Optimizing a Trainium2 kernel written in Bass

```python
import numpy as np
import jax
import jax.numpy as jnp

def _softmax(x, axis=-1):
    return jax.nn.softmax(x, axis=axis)

def _gelu(x):
    return jax.nn.gelu(x, approximate=True)

def _silu(x):
    return jax.nn.silu(x)

def _sigmoid(x):
    return jax.nn.sigmoid(x)

def _layernorm(x, axis=-1, eps=1e-05):
    m = jnp.mean(x, axis=axis, keepdims=True)
    v = jnp.var(x, axis=axis, keepdims=True)
    return (x - m) / jnp.sqrt(v + eps)

def _scatter_add(tgt, idx, src, axis=0):
    return tgt.at[idx].add(src)

def _segment_sum(src, seg, n):
    return jax.ops.segment_sum(src, seg, n)
kernel_name = 'mk_dlrm_tower_d1_rec_r8_9e22c7'

def setup_inputs(seed: int=0):
    np.random.seed(seed)
    _w = jnp.asarray

    def _rec_inputs():
        import jax
        import jax.numpy as jnp
        _tk = jax.random.key(seed)
        dense_ctx = jax.random.normal(jax.random.fold_in(_tk, 190), (2048, 16), jnp.float32)
        ids = jnp.stack([jax.random.randint(jax.random.fold_in(_tk, 200 + f), (2048,), 0, v, jnp.int32) for f, v in enumerate([1250, 1250, 12500, 1250, 1250, 12500, 1000, 12500, 1250, 12500, 1250, 125000, 12500, 125000, 1250, 12500, 125000, 125000, 12500, 125000, 1250, 1250, 12500, 1000, 12500, 125000, 1000, 12500, 1250, 12500, 1000, 1250, 1000, 12500, 1000, 1000, 1250, 12500, 1250, 1000])], axis=1)
        tbl_0 = 0.05 * jax.random.normal(jax.random.fold_in(_tk, 500 + 0), (1250, 32), jnp.float32)
        tbl_1 = 0.05 * jax.random.normal(jax.random.fold_in(_tk, 500 + 1), (1250, 32), jnp.float32)
        tbl_2 = 0.05 * jax.random.normal(jax.random.fold_in(_tk, 500 + 2), (12500, 32), jnp.float32)
        tbl_3 = 0.05 * jax.random.normal(jax.random.fold_in(_tk, 500 + 3), (1250, 32), jnp.float32)
        tbl_4 = 0.05 * jax.random.normal(jax.random.fold_in(_tk, 500 + 4), (1250, 32), jnp.float32)
        tbl_5 = 0.05 * jax.random.normal(jax.random.fold_in(_tk, 500 + 5), (12500, 32), jnp.float32)
        tbl_6 = 0.05 * jax.random.normal(jax.random.fold_in(_tk, 500 + 6), (1000, 32), jnp.float32)
        tbl_7 = 0.05 * jax.random.normal(jax.random.fold_in(_tk, 500 + 7), (12500, 32), jnp.float32)
        tbl_8 = 0.05 * jax.random.normal(jax.random.fold_in(_tk, 500 + 8), (1250, 32), jnp.float32)
        tbl_9 = 0.05 * jax.random.normal(jax.random.fold_in(_tk, 500 + 9), (12500, 32), jnp.float32)
        tbl_10 = 0.05 * jax.random.normal(jax.random.fold_in(_tk, 500 + 10), (1250, 32), jnp.float32)
        tbl_11 = 0.05 * jax.random.normal(jax.random.fold_in(_tk, 500 + 11), (125000, 32), jnp.float32)
        tbl_12 = 0.05 * jax.random.normal(jax.random.fold_in(_tk, 500 + 12), (12500, 32), jnp.float32)
        tbl_13 = 0.05 * jax.random.normal(jax.random.fold_in(_tk, 500 + 13), (125000, 32), jnp.float32)
        tbl_14 = 0.05 * jax.random.normal(jax.random.fold_in(_tk, 500 + 14), (1250, 32), jnp.float32)
        tbl_15 = 0.05 * jax.random.normal(jax.random.fold_in(_tk, 500 + 15), (12500, 32), jnp.float32)
        tbl_16 = 0.05 * jax.random.normal(jax.random.fold_in(_tk, 500 + 16), (125000, 32), jnp.float32)
        tbl_17 = 0.05 * jax.random.normal(jax.random.fold_in(_tk, 500 + 17), (125000, 32), jnp.float32)
        tbl_18 = 0.05 * jax.random.normal(jax.random.fold_in(_tk, 500 + 18), (12500, 32), jnp.float32)
        tbl_19 = 0.05 * jax.random.normal(jax.random.fold_in(_tk, 500 + 19), (125000, 32), jnp.float32)
        tbl_20 = 0.05 * jax.random.normal(jax.random.fold_in(_tk, 500 + 20), (1250, 32), jnp.float32)
        tbl_21 = 0.05 * jax.random.normal(jax.random.fold_in(_tk, 500 + 21), (1250, 32), jnp.float32)
        tbl_22 = 0.05 * jax.random.normal(jax.random.fold_in(_tk, 500 + 22), (12500, 32), jnp.float32)
        tbl_23 = 0.05 * jax.random.normal(jax.random.fold_in(_tk, 500 + 23), (1000, 32), jnp.float32)
        tbl_24 = 0.05 * jax.random.normal(jax.random.fold_in(_tk, 500 + 24), (12500, 32), jnp.float32)
        tbl_25 = 0.05 * jax.random.normal(jax.random.fold_in(_tk, 500 + 25), (125000, 32), jnp.float32)
        tbl_26 = 0.05 * jax.random.normal(jax.random.fold_in(_tk, 500 + 26), (1000, 32), jnp.float32)
        tbl_27 = 0.05 * jax.random.normal(jax.random.fold_in(_tk, 500 + 27), (12500, 32), jnp.float32)
        tbl_28 = 0.05 * jax.random.normal(jax.random.fold_in(_tk, 500 + 28), (1250, 32), jnp.float32)
        tbl_29 = 0.05 * jax.random.normal(jax.random.fold_in(_tk, 500 + 29), (12500, 32), jnp.float32)
        tbl_30 = 0.05 * jax.random.normal(jax.random.fold_in(_tk, 500 + 30), (1000, 32), jnp.float32)
        tbl_31 = 0.05 * jax.random.normal(jax.random.fold_in(_tk, 500 + 31), (1250, 32), jnp.float32)
        tbl_32 = 0.05 * jax.random.normal(jax.random.fold_in(_tk, 500 + 32), (1000, 32), jnp.float32)
        tbl_33 = 0.05 * jax.random.normal(jax.random.fold_in(_tk, 500 + 33), (12500, 32), jnp.float32)
        tbl_34 = 0.05 * jax.random.normal(jax.random.fold_in(_tk, 500 + 34), (1000, 32), jnp.float32)
        tbl_35 = 0.05 * jax.random.normal(jax.random.fold_in(_tk, 500 + 35), (1000, 32), jnp.float32)
        tbl_36 = 0.05 * jax.random.normal(jax.random.fold_in(_tk, 500 + 36), (1250, 32), jnp.float32)
        tbl_37 = 0.05 * jax.random.normal(jax.random.fold_in(_tk, 500 + 37), (12500, 32), jnp.float32)
        tbl_38 = 0.05 * jax.random.normal(jax.random.fold_in(_tk, 500 + 38), (1250, 32), jnp.float32)
        tbl_39 = 0.05 * jax.random.normal(jax.random.fold_in(_tk, 500 + 39), (1000, 32), jnp.float32)
        _rk = jax.random.fold_in(_tk, 7)
        W_top1 = 0.0354441 * jax.random.normal(jax.random.fold_in(_tk, 801), (796, 512), jnp.float32)
        W_top2 = 0.0441942 * jax.random.normal(jax.random.fold_in(_tk, 802), (512, 256), jnp.float32)
        W_top3 = 0.0625 * jax.random.normal(jax.random.fold_in(_tk, 803), (256, 1), jnp.float32)
        b_top1 = jnp.zeros((512,), jnp.float32)
        b_top2 = jnp.zeros((256,), jnp.float32)
        return (dense_ctx, ids, tbl_0, tbl_1, tbl_2, tbl_3, tbl_4, tbl_5, tbl_6, tbl_7, tbl_8, tbl_9, tbl_10, tbl_11, tbl_12, tbl_13, tbl_14, tbl_15, tbl_16, tbl_17, tbl_18, tbl_19, tbl_20, tbl_21, tbl_22, tbl_23, tbl_24, tbl_25, tbl_26, tbl_27, tbl_28, tbl_29, tbl_30, tbl_31, tbl_32, tbl_33, tbl_34, tbl_35, tbl_36, tbl_37, tbl_38, tbl_39, W_top1, b_top1, W_top2, b_top2, W_top3)
    dense_ctx, ids, tbl_0, tbl_1, tbl_2, tbl_3, tbl_4, tbl_5, tbl_6, tbl_7, tbl_8, tbl_9, tbl_10, tbl_11, tbl_12, tbl_13, tbl_14, tbl_15, tbl_16, tbl_17, tbl_18, tbl_19, tbl_20, tbl_21, tbl_22, tbl_23, tbl_24, tbl_25, tbl_26, tbl_27, tbl_28, tbl_29, tbl_30, tbl_31, tbl_32, tbl_33, tbl_34, tbl_35, tbl_36, tbl_37, tbl_38, tbl_39, W_top1, b_top1, W_top2, b_top2, W_top3 = _rec_inputs()

    def _L0_rec_setup():
        import jax, jax.numpy as jnp
        import numpy as np
        NUM_FIELDS = 40
        _I_IDX, _J_IDX = np.triu_indices(NUM_FIELDS, k=1)
        key = jax.random.key(seed)
        k1, k2 = jax.random.split(key)
        batch, num_fields, embed_dim = (1024, NUM_FIELDS, 32)
        num_interactions = num_fields * (num_fields - 1) // 2
        embeddings = jax.random.normal(k1, (batch, num_fields, embed_dim), dtype=jnp.float32)
        W = jax.random.normal(k2, (num_interactions, embed_dim, embed_dim), dtype=jnp.float32)
        return {'embeddings': embeddings, 'W': W}
    _L0_rec_all = _L0_rec_setup()
    _L0_rec_in = {k: v for k, v in _L0_rec_all.items() if k in ('W',)}
    del _L0_rec_all
    return {'dense_ctx': dense_ctx, 'ids': ids, 'tbl_0': tbl_0, 'tbl_1': tbl_1, 'tbl_2': tbl_2, 'tbl_3': tbl_3, 'tbl_4': tbl_4, 'tbl_5': tbl_5, 'tbl_6': tbl_6, 'tbl_7': tbl_7, 'tbl_8': tbl_8, 'tbl_9': tbl_9, 'tbl_10': tbl_10, 'tbl_11': tbl_11, 'tbl_12': tbl_12, 'tbl_13': tbl_13, 'tbl_14': tbl_14, 'tbl_15': tbl_15, 'tbl_16': tbl_16, 'tbl_17': tbl_17, 'tbl_18': tbl_18, 'tbl_19': tbl_19, 'tbl_20': tbl_20, 'tbl_21': tbl_21, 'tbl_22': tbl_22, 'tbl_23': tbl_23, 'tbl_24': tbl_24, 'tbl_25': tbl_25, 'tbl_26': tbl_26, 'tbl_27': tbl_27, 'tbl_28': tbl_28, 'tbl_29': tbl_29, 'tbl_30': tbl_30, 'tbl_31': tbl_31, 'tbl_32': tbl_32, 'tbl_33': tbl_33, 'tbl_34': tbl_34, 'tbl_35': tbl_35, 'tbl_36': tbl_36, 'tbl_37': tbl_37, 'tbl_38': tbl_38, 'tbl_39': tbl_39, 'W_top1': W_top1, 'b_top1': b_top1, 'W_top2': W_top2, 'b_top2': b_top2, 'W_top3': W_top3, 'L0_rec_W': _L0_rec_in['W']}

def reference(dense_ctx, ids, tbl_0, tbl_1, tbl_2, tbl_3, tbl_4, tbl_5, tbl_6, tbl_7, tbl_8, tbl_9, tbl_10, tbl_11, tbl_12, tbl_13, tbl_14, tbl_15, tbl_16, tbl_17, tbl_18, tbl_19, tbl_20, tbl_21, tbl_22, tbl_23, tbl_24, tbl_25, tbl_26, tbl_27, tbl_28, tbl_29, tbl_30, tbl_31, tbl_32, tbl_33, tbl_34, tbl_35, tbl_36, tbl_37, tbl_38, tbl_39, W_top1, b_top1, W_top2, b_top2, W_top3, L0_rec_W):
    import jax
    import jax.numpy as jnp

    def _L0_rec_ref(embeddings, W):
        import jax, jax.numpy as jnp
        import numpy as np
        NUM_FIELDS = 40
        _I_IDX, _J_IDX = np.triu_indices(NUM_FIELDS, k=1)
        vi = embeddings[:, _I_IDX, :]
        vj = embeddings[:, _J_IDX, :]
        return jnp.einsum('bke,kef,bkf->bk', vi, W, vj)
    e = jnp.stack([tbl_0[ids[:, 0]], tbl_1[ids[:, 1]], tbl_2[ids[:, 2]], tbl_3[ids[:, 3]], tbl_4[ids[:, 4]], tbl_5[ids[:, 5]], tbl_6[ids[:, 6]], tbl_7[ids[:, 7]], tbl_8[ids[:, 8]], tbl_9[ids[:, 9]], tbl_10[ids[:, 10]], tbl_11[ids[:, 11]], tbl_12[ids[:, 12]], tbl_13[ids[:, 13]], tbl_14[ids[:, 14]], tbl_15[ids[:, 15]], tbl_16[ids[:, 16]], tbl_17[ids[:, 17]], tbl_18[ids[:, 18]], tbl_19[ids[:, 19]], tbl_20[ids[:, 20]], tbl_21[ids[:, 21]], tbl_22[ids[:, 22]], tbl_23[ids[:, 23]], tbl_24[ids[:, 24]], tbl_25[ids[:, 25]], tbl_26[ids[:, 26]], tbl_27[ids[:, 27]], tbl_28[ids[:, 28]], tbl_29[ids[:, 29]], tbl_30[ids[:, 30]], tbl_31[ids[:, 31]], tbl_32[ids[:, 32]], tbl_33[ids[:, 33]], tbl_34[ids[:, 34]], tbl_35[ids[:, 35]], tbl_36[ids[:, 36]], tbl_37[ids[:, 37]], tbl_38[ids[:, 38]], tbl_39[ids[:, 39]]], axis=1)
    z = _L0_rec_ref(e, L0_rec_W)
    z = z.reshape(z.shape[0], -1)
    h = jnp.concatenate([z, dense_ctx], axis=1)
    h = jnp.maximum(h @ W_top1 + b_top1, 0.0)
    h = jnp.maximum(h @ W_top2 + b_top2, 0.0)
    y = h @ W_top3
    return y

_drawn_inputs = setup_inputs


def setup_inputs(seed=0):
    import zlib

    import numpy as np

    out = dict(_drawn_inputs(seed))
    spreads = {'b_top1': (0.0, 0.1), 'b_top2': (0.0, 0.1)}
    factors = {}
    for name, (base, spread) in spreads.items():
        noise = np.random.default_rng([zlib.crc32(name.encode()), seed]).standard_normal(out[name].shape)
        drawn = base * np.exp(spread * noise) if base else spread * noise
        out[name] = jnp.asarray(drawn.astype(out[name].dtype))
    for name, factor in factors.items():
        out[name] = (out[name] * factor).astype(out[name].dtype)
    return out
```

```python
from contextlib import ExitStack

import concourse.bass as bass
from concourse import mybir

F32 = mybir.dt.float32
F32R = mybir.dt.float32r
I32 = mybir.dt.int32
ALU = mybir.AluOpType
ACT = mybir.ActivationFunctionType

P = 128
BATCH, FIELDS, EMB = 2048, 40, 32
DENSE = 16
H1, H2 = 512, 256
CHUNK = 256
TILES = CHUNK // P
CHUNKS = BATCH // CHUNK
GROUP = 8
GROUPS = FIELDS // GROUP
LO = P // GROUP
HI = EMB // LO
SOURCES = FIELDS // 2

ORDER = [1, 0] + list(range(2, SOURCES))
QUADS = [(n, m, t, 2 * m % GROUP == 0 and t == 2 * m // GROUP)
         for n, m in enumerate(ORDER) for t in range(2 * m // GROUP + 1)]
NQ = len(QUADS)
START = [min(q for q, x in enumerate(QUADS) if x[0] == n) for n in range(SOURCES)]
END = [max(q for q, x in enumerate(QUADS) if x[0] == n) for n in range(SOURCES)]
G_START = [START[GROUP // 2 * g] for g in range(GROUPS)]
G_LAST = [max(q for q, x in enumerate(QUADS) if x[2] == g) for g in range(GROUPS)]

BLOCKS = [(q, s, h) for q, x in enumerate(QUADS) for s in range(2) if s or not x[3] for h in range(HI)]
BLOCK_AT = {b: n for n, b in enumerate(BLOCKS)}
NB = len(BLOCKS)
PIECE = 8
PIECES = -(-NB // PIECE)

ZQ = P // GROUP
Z_TILES = -(-NQ // ZQ)
Z_END = [min(ZQ * (k + 1), NQ) for k in range(Z_TILES)]
DENSE_ROW = GROUP * (NQ % ZQ)
O1, O2 = H1 // P, H2 // P

LAG = 3
T1_AT = 3
T2_AT = 8
T3_AT = 17
assert NQ % 6 == 0 and DENSE_ROW % 32 == 0 and DENSE_ROW + DENSE <= P and DENSE_ROW


def field_prep():
    prep = []
    for n in range(SOURCES):
        back = START[n - 1] if n else START[-1] - NQ
        if n % (GROUP // 2) == 0:
            prep.append((START[n] - 3, "V", n // (GROUP // 2)))
            prep.append((START[n] - 2, "E", n))
        else:
            prep.append((max(back, START[n] - 3), "E", n))
    return sorted(prep, key=lambda x: x[0])


PREP = field_prep()


def prep_at(pos):
    for place, (p, kind, i) in enumerate(PREP):
        if p == pos:
            yield 0, kind, i, place
        if p + NQ == pos:
            yield 1, kind, i, place


def splits_at(pos):
    for g in range(GROUPS):
        if G_START[g] - 4 == pos:
            yield 0, g
        if G_START[g] - 4 + NQ == pos:
            yield 1, g


def pieces_at(pos):
    def upto(p):
        last = min(p + 4, NQ - 1)
        return BLOCK_AT[(last, 1, HI - 1)] // PIECE + 1
    return range(upto(pos - 1) if pos else 0, upto(pos))


def build(nc, ids, tables, w, dense, w1, b1, w2, b2, w3, ident, staircase, out):
    with ExitStack() as ctx:
        def sb(name, shape, dt=F32):
            return ctx.enter_context(nc.sbuf_tensor(name, shape, dt))

        def psum(name, shape):
            return ctx.enter_context(nc.psum_tensor(name, shape, F32))

        def sem(name):
            return ctx.enter_context(nc.semaphore(name))

        w_sb = sb("w_sb", [P, NB, P])
        stage = sb("stage", [P, 2, PIECE * P])
        ids_all = sb("ids_all", [P, CHUNKS * TILES * FIELDS], I32)
        ids_now = sb("ids_now", [P, TILES, FIELDS], I32)
        raw = sb("raw", [P, TILES, FIELDS, EMB])
        hl = sb("hl", [P, 2, TILES, GROUP, 2, EMB])
        et = sb("et", [P, 2, 2, CHUNK])
        v = sb("v", [P, GROUPS, HI, CHUNK])
        prod = sb("prod", [P, 3, 2, HI, CHUNK])
        s_sb = sb("s_sb", [P, 2, 2, CHUNK])
        zt = sb("zt", [P, 2, 2, CHUNK])
        w1_sb = sb("w1_sb", [P, Z_TILES, 2, H1])
        w2_sb = sb("w2_sb", [P, O1, H2])
        w3_sb = sb("w3_sb", [P, O2])
        b1_sb = sb("b1_sb", [P, O1])
        b2_sb = sb("b2_sb", [P, O2])
        h1_sb = sb("h1_sb", [P, O1, CHUNK])
        h2_sb = sb("h2_sb", [P, O2, CHUNK])
        y_sb = sb("y_sb", [1, CHUNK])
        id_sb = sb("id_sb", [P, P])
        stair = sb("stair", [P, 2 * P - GROUP])

        a_ps = psum("a_ps", [P, 2, 2, HI, CHUNK])
        z_ps = psum("z_ps", [P, 2, CHUNK])
        t_ps = psum("t_ps", [P, 2, CHUNK])
        h_ps = psum("h_ps", [P, O1, CHUNK])

        const_in = sem("const_in")
        ids_in = sem("ids_in")
        top_in = sem("top_in")
        w_in = [sem(f"w_in{i}") for i in range(2)]
        ids_copied = sem("ids_copied")
        rows_free = sem("rows_free")
        gathered = [sem(f"gathered{g}") for g in range(GROUPS)]
        w_rounded = sem("w_rounded")
        w_ready = sem("w_ready")
        h_split = sem("h_split")
        l_split = sem("l_split")
        v_transposed = sem("v_transposed")
        e_transposed = sem("e_transposed")
        v_ready = sem("v_ready")
        e_ready = sem("e_ready")
        a_ready = sem("a_ready")
        multiplied = sem("multiplied")
        s_ready = sem("s_ready")
        summed = sem("summed")
        z_ready = sem("z_ready")
        dense_in = sem("dense_in")
        top1_done = sem("top1_done")
        h1_ready = sem("h1_ready")
        top2_done = sem("top2_done")
        h2_ready = sem("h2_ready")
        top3_done = sem("top3_done")
        y_ready = sem("y_ready")
        y_out = sem("y_out")
        y_free = sem("y_free")

        def chunks(eng, body, tail):
            body(0, True, False)
            with eng.Fori(1, CHUNKS - 1) as c:
                body(c, False, False)
            body(CHUNKS - 1, False, True)
            tail(CHUNKS)

        block = ctx.enter_context(nc.Block())

        @block.sync
        def _(sp):
            sp.dma_start(ids_all[:], ids).then_inc(ids_in, 16)
            for p in range(PIECES):
                if p >= 2:
                    sp.wait_ge(w_ready, p - 1)
                n = min(PIECE, NB - p * PIECE) * P
                for copy in range(4):
                    sp.dma_start(stage[32 * copy:32 * copy + 32, p % 2, 0:n],
                                 w[:, p * PIECE * P:p * PIECE * P + n]).then_inc(w_in[p % 2], 16)

            def dense_of(c):
                sp.wait_ge(top1_done, c * Z_TILES + 2)
                sp.dma_start(zt[DENSE_ROW:DENSE_ROW + DENSE, 1, 0, :],
                             dense[:, bass.ds(c * CHUNK, CHUNK)]).then_inc(dense_in, 16)

            def result_of(c):
                sp.wait_ge(y_ready, c + 1)
                sp.dma_start(out[:, bass.ds(c * CHUNK, CHUNK)], y_sb[:]).then_inc(y_out, 16)
                sp.wait_ge(y_out, 16 * (c + 1))
                sp.sem_inc(y_free, 1)

            sp.sem_inc(y_free, 1)
            dense_of(0)
            with sp.Fori(1, CHUNKS) as c:
                result_of(c - 1)
                dense_of(c)
            result_of(CHUNKS - 1)

        @block.gpsimd
        def _(pool):
            def body(c, first):
                if not first:
                    for g in range(GROUPS):
                        pool.wait_ge(gathered[g], 16 * TILES * GROUP * c)
                nc.gpsimd.tensor_copy(ids_now[:].rearrange("p t f -> p (t f)"),
                                      ids_all[:, bass.ds(c * TILES * FIELDS, TILES * FIELDS)]).then_inc(ids_copied, 1)
                pool.wait_ge(ids_copied, c + 1)
                for g in range(GROUPS):
                    if not first:
                        pool.wait_ge(l_split, GROUPS * (c - 1) + g + 1)
                        pool.wait_ge(v_transposed, GROUPS * (c - 1) + g + 1)
                    pool.sem_inc(rows_free, 1)
                    for t in range(TILES):
                        for f in range(GROUP * g, GROUP * g + GROUP):
                            pool.indirect_dma_start(
                                out=raw[:, t, f, :], out_offset=None, in_=tables[f],
                                in_offset=bass.IndirectOffsetOnAxis(ap=ids_now[:, t, f:f + 1], axis=0),
                            ).then_inc(gathered[g], 16)

            pool.wait_ge(ids_in, 16)
            body(0, True)
            with pool.Fori(1, CHUNKS) as c:
                body(c, False)

        @block.tensor
        def _(pe):
            mm = nc.tensor.matmul

            def transposes(c, kind, i, place, first):
                if not (first and place == 0):
                    k = PREP[place - 1][1]
                    idx = PREP[place - 1][2]
                    cc = c if place else c - 1
                    if k == "V":
                        pe.wait_ge(v_ready, GROUPS * cc + idx + 1)
                    else:
                        pe.wait_ge(e_ready, SOURCES * cc + idx + 1)
                if kind == "V":
                    pe.wait_ge(gathered[i], 16 * TILES * GROUP * (c + 1))
                    for h in range(HI):
                        for t in range(TILES):
                            fields = raw[:, t, GROUP * i:GROUP * i + GROUP, :].rearrange("p f e -> p (f e)")
                            last = nc.tensor.transpose(
                                t_ps[:, h, P * t:P * t + P],
                                fields[:, h::HI], id_sb[:])
                    last.then_inc(v_transposed, 1)
                else:
                    g = ORDER[i] * 2 // GROUP
                    pe.wait_ge(l_split, GROUPS * c + g + 1)
                    j = 2 * ORDER[i] % GROUP
                    for t in range(TILES):
                        pair = hl[:, g % 2, t, j:j + 2].rearrange("p j s e -> p (j s e)")
                        last = nc.tensor.transpose(t_ps[:, 0, P * t:P * t + P], pair, id_sb[:])
                    last.then_inc(e_transposed, 1)

            def a_of(c, q, first):
                n, m, t, half = QUADS[q]
                if not (first and q < 2):
                    pe.wait_ge(multiplied, NQ * c + q - 1)
                if q == START[n]:
                    pe.wait_ge(e_ready, SOURCES * c + n + 1)
                if first:
                    pe.wait_ge(w_ready, BLOCK_AT[(q, 1, HI - 1)] // PIECE + 1)
                for s in range(half, 2):
                    for h in range(HI):
                        last = mm(a_ps[:, q % 2, s, h, :],
                                  w_sb[:, BLOCK_AT[(q, s, h)], :].bitcast(F32R),
                                  et[:, n % 2, s, :].bitcast(F32R), start=True, stop=True)
                last.then_inc(a_ready, 1)

            def sum_of(c, q, first):
                half = int(QUADS[q][3])
                pe.wait_ge(s_ready, NQ * c + q + 1)
                k = q // ZQ
                if q % ZQ == 0 and not (first and k == 0):
                    pe.wait_ge(z_ready, Z_TILES * c + k)
                at = P - GROUP - GROUP * (q % ZQ)
                mm(z_ps[:, half:2, :], stair[:, at:at + P], s_sb[:, q % 2, half:2, :],
                   start=q % ZQ == 0, stop=q + 1 == Z_END[k], skip_group_check=True).then_inc(summed, 1)

            def top1(c, k, unit, first):
                s, o = divmod(unit, O1)
                if unit == 0:
                    pe.wait_ge(z_ready, Z_TILES * c + k + 1)
                    if k == 0:
                        if first:
                            pe.wait_ge(top_in, 16 * 5)
                        else:
                            pe.wait_ge(y_ready, c)
                    if k == Z_TILES - 1:
                        pe.wait_ge(dense_in, 16 * (c + 1))
                rows = P if k < Z_TILES - 1 else DENSE_ROW if s else DENSE_ROW + DENSE
                last = mm(h_ps[:, o, :], w1_sb[0:rows, k, s, P * o:P * o + P], zt[0:rows, k % 2, s, :],
                          start=k == 0 and s == 0 and o % 2 == 0, stop=k == Z_TILES - 1 and s == 1,
                          skip_group_check=True)
                if unit == 2 * O1 - 1:
                    last.then_inc(top1_done, 1)

            def top2(c, unit):
                o, k = divmod(unit, O1)
                if unit == 0:
                    pe.wait_ge(h1_ready, O1 * (c + 1))
                last = mm(h_ps[:, o, :], w2_sb[:, k, P * o:P * o + P], h1_sb[:, k, :],
                          start=k == 0, stop=k == O1 - 1)
                if k == O1 - 1:
                    last.then_inc(top2_done, 1)

            def top3(c):
                pe.wait_ge(h2_ready, O2 * (c + 1))
                for k in range(O2):
                    last = mm(h_ps[0:1, 2, :], w3_sb[:, k:k + 1], h2_sb[:, k, :], start=k == 0, stop=k == O2 - 1)
                last.then_inc(top3_done, 1)

            def rest(c, pos, first):
                if pos < LAG:
                    sum_of(c - 1, NQ + pos - LAG, False)
                for unit in range(2 * O1):
                    if pos == T1_AT + unit // 2:
                        top1(c - 1, Z_TILES - 1, unit, False)
                if T2_AT <= pos < T2_AT + O1 * O2:
                    top2(c - 1, pos - T2_AT)
                if pos == T3_AT:
                    top3(c - 1)

            def body(c, first, final):
                if first:
                    for p, kind, i in PREP:
                        if p < 0:
                            transposes(0, kind, i, PREP.index((p, kind, i)), True)
                for pos in range(NQ):
                    for ahead, kind, i, place in prep_at(pos):
                        if not (ahead and final):
                            transposes(c + ahead, kind, i, place, False)
                    a_of(c, pos, first)
                    if not first:
                        rest(c, pos, first)
                    if pos >= LAG:
                        sum_of(c, pos - LAG, first)
                    for k in range(Z_TILES - 1):
                        unit = pos - (Z_END[k] + T1_AT)
                        if 0 <= unit < 2 * O1:
                            top1(c, k, unit, first)

            def tail(c):
                for pos in range(T3_AT + 1):
                    rest(c, pos, False)

            pe.wait_ge(const_in, 32)
            chunks(pe, body, tail)

        @block.scalar
        def _(act):
            copy = nc.scalar.activation

            def split_hi(c, g, first):
                act.wait_ge(gathered[g], 16 * TILES * GROUP * (c + 1))
                n = GROUP // 2 * (g - 1) if g >= 2 else 0
                if g >= 2:
                    act.wait_ge(e_transposed, SOURCES * c + n)
                elif not first:
                    act.wait_ge(e_transposed, SOURCES * c if g == 0 else SOURCES * c - GROUP // 2)
                copy(hl[:, g % 2, :, :, 0, :].bitcast(F32R), raw[:, :, GROUP * g:GROUP * g + GROUP, :],
                     ACT.Copy).then_inc(h_split, 1)

            def evacuate(c, kind, i, first):
                if kind == "V":
                    act.wait_ge(v_transposed, GROUPS * c + i + 1)
                    if not first:
                        act.wait_ge(multiplied, NQ * (c - 1) + G_LAST[i] + 1)
                    copy(v[:, i], t_ps[:], ACT.Copy).then_inc(v_ready, 1)
                else:
                    act.wait_ge(e_transposed, SOURCES * c + i + 1)
                    if i >= 2:
                        act.wait_ge(a_ready, NQ * c + END[i - 2] + 1)
                    elif not first:
                        act.wait_ge(a_ready, NQ * (c - 1) + END[SOURCES + i - 2] + 1)
                    for s in range(2):
                        for half in range(2):
                            last = copy(et[64 * half:64 * half + 64, i % 2, s, :].bitcast(F32R),
                                        t_ps[64 * s:64 * s + 64, 0, :], ACT.Copy)
                    last.then_inc(e_ready, 1)

            def z_of(c, k, first):
                act.wait_ge(summed, NQ * c + Z_END[k])
                if not (first and k < 2):
                    act.wait_ge(top1_done, Z_TILES * c + k - 1)
                rows = P if k < Z_TILES - 1 else DENSE_ROW
                copy(zt[0:rows, k % 2], z_ps[0:rows], ACT.Copy).then_inc(z_ready, 1)

            def rest(c, pos):
                if pos == LAG - 1:
                    z_of(c - 1, Z_TILES - 1, False)
                if pos == T2_AT - 1:
                    act.wait_ge(top1_done, Z_TILES * c)
                    for o in range(O1):
                        copy(h1_sb[:, o, :], h_ps[:, o, :], ACT.Relu, bias=b1_sb[:, o:o + 1]).then_inc(h1_ready, 1)
                if pos == T3_AT - 1:
                    act.wait_ge(top2_done, O2 * c)
                    for o in range(O2):
                        copy(h2_sb[:, o, :], h_ps[:, o, :], ACT.Relu, bias=b2_sb[:, o:o + 1]).then_inc(h2_ready, 1)
                if pos == T3_AT:
                    act.wait_ge(top3_done, c)
                    result(c)

            def result(c):
                act.wait_ge(y_free, c)
                copy(y_sb[:], h_ps[0:1, 2, :], ACT.Copy).then_inc(y_ready, 1)

            def body(c, first, final):
                if first:
                    split_hi(0, 0, True)
                    for p, kind, i in PREP:
                        if p < 0:
                            evacuate(0, kind, i, True)
                for pos in range(NQ):
                    if first:
                        for p in pieces_at(pos):
                            act.wait_ge(w_in[p % 2], 64 * (p // 2 + 1))
                            n = min(PIECE, NB - p * PIECE)
                            copy(w_sb[:, PIECE * p:PIECE * p + n, :].bitcast(F32R),
                                 stage[:, p % 2, 0:n * P].rearrange("p (n c) -> p n c", c=P),
                                 ACT.Copy).then_inc(w_rounded, 1)
                    for ahead, g in splits_at(pos):
                        if not (ahead and final):
                            split_hi(c + ahead, g, first and not ahead)
                    for ahead, kind, i, _ in prep_at(pos):
                        if not (ahead and final):
                            evacuate(c + ahead, kind, i, first and not ahead)
                    if not first:
                        rest(c, pos)
                    for k in range(Z_TILES - 1):
                        if pos == Z_END[k] - 1 + LAG:
                            z_of(c, k, first)

            def tail(c):
                for pos in range(T3_AT + 1):
                    rest(c, pos)

            act.dma_start(id_sb[:], ident).then_inc(const_in, 16)
            act.dma_start(stair[:], staircase).then_inc(const_in, 16)
            act.dma_start(b1_sb[:], b1).then_inc(top_in, 16)
            act.dma_start(b2_sb[:], b2).then_inc(top_in, 16)
            act.dma_start(w3_sb[:], w3).then_inc(top_in, 16)
            act.dma_start(w2_sb[:], w2).then_inc(top_in, 16)
            act.dma_start(w1_sb[:], w1).then_inc(top_in, 16)
            chunks(act, body, tail)

        @block.vector
        def _(dve):
            tt = nc.vector.tensor_tensor

            def split_lo(c, g):
                dve.wait_ge(h_split, GROUPS * c + g + 1)
                tt(hl[:, g % 2, :, :, 1, :].bitcast(F32R), raw[:, :, GROUP * g:GROUP * g + GROUP, :],
                   hl[:, g % 2, :, :, 0, :], ALU.subtract).then_inc(l_split, 1)

            def multiply(c, q, first):
                n, m, t, half = QUADS[q]
                if not (first and q < 3):
                    dve.wait_ge(s_ready, NQ * c + q - 2)
                dve.wait_ge(a_ready, NQ * c + q + 1)
                if q == min(i for i, x in enumerate(QUADS) if x[2] == t):
                    dve.wait_ge(v_ready, GROUPS * c + t + 1)
                k = 2 - half
                tt(prod[:, q % 3, half:2].rearrange("p s h b -> p s (h b)"),
                   a_ps[:, q % 2, half:2].rearrange("p s h b -> p s (h b)"),
                   v[:, t].rearrange("p h b -> p (h b)").unsqueeze(1).broadcast_to([P, k, HI * CHUNK]),
                   ALU.mult).then_inc(multiplied, 1)

            def add(c, q, first):
                half = int(QUADS[q][3])
                dve.wait_ge(multiplied, NQ * c + q + 1)
                if not (first and q < 2):
                    dve.wait_ge(summed, NQ * c + q - 1)
                tt(s_sb[:, q % 2, half:2], prod[:, q % 3, half:2, 0, :], prod[:, q % 3, half:2, 1, :],
                   ALU.add).then_inc(s_ready, 1)

            def body(c, first, final):
                if first:
                    split_lo(0, 0)
                for pos in range(NQ):
                    if first:
                        for p in pieces_at(pos):
                            dve.wait_ge(w_rounded, p + 1)
                            n = min(PIECE, NB - p * PIECE)
                            lo = w_sb[P // 2:P, PIECE * p:PIECE * p + n, :]
                            tt(lo.bitcast(F32R),
                               stage[P // 2:P, p % 2, 0:n * P].rearrange("p (n c) -> p n c", c=P),
                               lo, ALU.subtract).then_inc(w_ready, 1)
                    for ahead, g in splits_at(pos):
                        if not (ahead and final):
                            split_lo(c + ahead, g)
                    multiply(c, pos, first)
                    if pos:
                        add(c, pos - 1, first)
                    elif not first:
                        add(c - 1, NQ - 1, False)

            def tail(c):
                add(c - 1, NQ - 1, False)

            chunks(dve, body, tail)


def kernel(**inputs):
    import numpy as np
    import concourse.bacc as bacc
    from concourse.bass_utils import run_bass_kernel_spmd

    nc = bacc.Bacc("TRN2", target_bir_lowering=False, num_devices=1)
    arrays = {}

    def given(name, a):
        arrays[name] = np.ascontiguousarray(a)
        return nc.dram_tensor(name, a.shape, mybir.dt.from_np(a.dtype), kind="ExternalInput").ap()

    i_of, j_of = np.triu_indices(FIELDS, k=1)
    pair = -np.ones((FIELDS, FIELDS), np.int64)
    pair[i_of, j_of] = np.arange(len(i_of))

    ids = np.asarray(inputs["ids"]).reshape(CHUNKS * TILES, P, FIELDS).transpose(1, 0, 2).reshape(P, -1)

    w_in = np.asarray(inputs["L0_rec_W"])
    w = np.zeros((EMB, NB, GROUP, LO), w_in.dtype)
    w1_in = np.asarray(inputs["W_top1"])
    w1 = np.zeros((P, Z_TILES, 2, H1), w1_in.dtype)
    for (q, s, h), n in BLOCK_AT.items():
        _, m, t, _ = QUADS[q]
        for u in range(GROUP):
            k = pair[GROUP * t + u, 2 * m + s] if GROUP * t + u < 2 * m + s else -1
            if k >= 0:
                w[:, n, u, :] = w_in[k, h::HI, :].T
                w1[GROUP * (q % ZQ) + u, q // ZQ, s] = w1_in[k]
    w1[DENSE_ROW:DENSE_ROW + DENSE, Z_TILES - 1, 0] = w1_in[len(i_of):]

    stair = np.zeros((P, 2 * P - GROUP), np.float32)
    stair[np.arange(P), P - GROUP + np.arange(P) // LO] = 1

    args = [
        given("ids_d", ids),
        [given(f"tbl_{f}_d", np.asarray(inputs[f"tbl_{f}"])) for f in range(FIELDS)],
        given("w_d", w.reshape(EMB, -1)),
        given("dense_d", np.asarray(inputs["dense_ctx"]).T),
        given("w_top1_d", w1),
        given("b_top1_d", np.asarray(inputs["b_top1"]).reshape(O1, P).T),
        given("w_top2_d", np.asarray(inputs["W_top2"]).reshape(O1, P, H2).transpose(1, 0, 2)),
        given("b_top2_d", np.asarray(inputs["b_top2"]).reshape(O2, P).T),
        given("w_top3_d", np.asarray(inputs["W_top3"]).reshape(O2, P).T),
        given("ident_d", np.eye(P, dtype=np.float32)),
        given("stair_d", stair),
    ]
    y = nc.dram_tensor("y_d", (1, BATCH), F32, kind="ExternalOutput").ap()
    build(nc, *args, y)
    r = run_bass_kernel_spmd(nc, [arrays], core_ids=[0])
    return r.results[0]["y_d"].reshape(BATCH, 1)
```

```python
from contextlib import ExitStack

import concourse.bass as bass
from concourse import mybir

F32 = mybir.dt.float32
F32R = mybir.dt.float32r
I32 = mybir.dt.int32
ALU = mybir.AluOpType
ACT = mybir.ActivationFunctionType

P = 128
BATCH, FIELDS, EMB = 2048, 40, 32
DENSE = 16
H1, H2 = 512, 256
CHUNK = 256
TILES = CHUNK // P
CHUNKS = BATCH // CHUNK
GROUP = 8
GROUPS = FIELDS // GROUP
LO = P // GROUP
HI = EMB // LO
SOURCES = FIELDS // 2

HALF = GROUP // 2
MIX_A, MIX_B = GROUPS, GROUPS + 1
MIXED = 4


def tile_fields(tile, double):
    if tile < GROUPS:
        return [GROUP * tile + u for u in range(GROUP)]
    first = 2 * GROUP * double
    low = first + (HALF if tile == MIX_A else 0)
    return [first + GROUP + u for u in range(HALF)] + [low + u for u in range(HALF)]


def plan():
    order, quads, met = [], [], set()
    work = []
    for g in range(GROUPS):
        ms = [HALF * g + u for u in range(HALF)]
        if g < MIXED:
            tiles = [[g], [MIX_A]] if g % 2 == 0 else [[MIX_B], [g - 1, g]]
            low, high = ms[:2], ms[2:]
            work += [(m, tiles[0]) for m in low]
            work += [(m, tiles[1]) for m in high[::-1]]
        else:
            work += [(m, [g]) for m in ms]
    for m, own in work:
        double = m // GROUP
        before = list(range(2 * double)) if HALF * MIXED > m else list(range(MIXED))
        for tile in before + own:
            slots = {}
            for s in (1, 0):
                for u, i in enumerate(tile_fields(tile, double)):
                    j = 2 * m + s
                    if i != j and frozenset((i, j)) not in met:
                        met.add(frozenset((i, j)))
                        slots[u, s] = i, j
            quads.append((len(order), m, tile, slots))
        order.append(m)
    assert len(met) == FIELDS * (FIELDS - 1) // 2
    return order, quads


ORDER, QUADS = plan()
NQ = len(QUADS)
ODD = [int(all(s for _, s in x[3])) for x in QUADS]
START = [min(q for q, x in enumerate(QUADS) if x[0] == n) for n in range(SOURCES)]
END = [max(q for q, x in enumerate(QUADS) if x[0] == n) for n in range(SOURCES)]
G_START = [START[HALF * g] for g in range(GROUPS)]


def first_use(tile, after=0):
    return min(q for q in range(after, NQ) if QUADS[q][2] == tile)


def last_use(tile, before=NQ):
    return max((q for q in range(before) if QUADS[q][2] == tile), default=None)


NEEDS = [tile if tile < GROUPS else m // GROUP * 2 + 1 for _, m, tile, _ in QUADS]


BLOCKS = [(q, s, h) for q in range(NQ) for s in range(ODD[q], 2) for h in range(HI)]
BLOCK_AT = {b: n for n, b in enumerate(BLOCKS)}
NB = len(BLOCKS)
PART = 8
QUARTERS = P // EMB
PIECE = QUARTERS * PART
PIECES = -(-NB // PIECE)
PIECE_POS = [-1, -1, 0, 1, 4, 6, 14]


def rows_of_z():
    at, tile, row = [], 0, 0
    for _, _, _, slots in QUADS:
        low, high = min(u for u, _ in slots), max(u for u, _ in slots) + 1
        if row + high - low > P:
            tile, row = tile + 1, 0
        at.append((tile, row - low))
        row += high - low
    return at, row


Z_AT, LAST_ROWS = rows_of_z()
Z_TILES = Z_AT[-1][0] + 1
Z_START = [min(q for q in range(NQ) if Z_AT[q][0] == k) for k in range(Z_TILES)]
Z_END = [max(q for q in range(NQ) if Z_AT[q][0] == k) + 1 for k in range(Z_TILES)]
ODD_ROW = P // 2
DENSE_ROW = ODD_ROW - DENSE
assert LAST_ROWS <= DENSE_ROW
K_BLOCKS = [(k, s) for k in range(Z_TILES - 1) for s in range(2)] + [(Z_TILES - 1, 0)]
O1, O2 = H1 // P, H2 // P

LAG = 3
PRODS = 3
T1_AT = [[38, 39, 40, 41, 43, 44, 45, 46], [47, 48, 49, 51, 53, 54, 55, 56],
         [NQ + p for p in (5, 7, 8, 10, 11, 13, 14, 16)], [NQ + p for p in (17, 19, 20, 21)]]
T1_AT_FINAL = T1_AT[:2] + [[54 + p for p in range(8)], [62 + p for p in range(4)]]
H1_AT, T2_AT, H2_AT, T3_AT = 22, [25, 26, 27, 28, 29, 30, 31, 33], 34, 36
assert NQ % 2 == 0 and SOURCES % 4 == 0 and Z_TILES == 4
assert all(at[0] > end + LAG for at, end in zip(T1_AT, Z_END))
assert T1_AT[3][-1] < NQ + H1_AT < NQ + T2_AT[0] and T2_AT[-1] < H2_AT < T3_AT < T1_AT[0][0] - 1
assert T1_AT[0][-1] < Z_END[2] + LAG and T1_AT[2][-1] < NQ + Z_END[0] + LAG
assert T1_AT[1][-1] < Z_END[3] + LAG and T1_AT[3][-1] < NQ + Z_END[1] + LAG


V_POS = [-4, -2, 9, 15, 35]
V_POS_FIRST = [-4, 1, 9, 15, 35]
DOUBLES = SOURCES // 2


def field_prep(v_pos):
    prep = [(p, "V", g) for g, p in enumerate(v_pos)] + [(-6, "E", 0)]
    prep += [(max(START[2 * d - 2] - 1, START[2 * d] - 4), "E", d) for d in range(1, DOUBLES)]
    return sorted(prep, key=lambda x: x[0])


SPLIT_POS = [-8, 0, 4, 16, 30]
PREP = field_prep(V_POS)
PREP_FIRST = field_prep(V_POS_FIRST)
assert PREP[-1] == PREP_FIRST[-1]


def prep_at(pos, first):
    for place, (p, kind, i) in enumerate(PREP_FIRST if first else PREP):
        if p == pos:
            yield 0, kind, i, ((PREP_FIRST if first else PREP)[place - 1] if place else None)
    for place, (p, kind, i) in enumerate(PREP):
        if p + NQ == pos:
            yield 1, kind, i, (PREP[place - 1] if place else None)


def splits_at(pos):
    for g in range(GROUPS):
        if SPLIT_POS[g] == pos:
            yield 0, g
        if SPLIT_POS[g] + NQ == pos:
            yield 1, g


def pieces_at(pos):
    return [p for p in range(PIECES) if PIECE_POS[p] == pos]


assert all(PIECE_POS[BLOCK_AT[q, 1, HI - 1] // PIECE] <= q for q in range(NQ))


GATHERS = FIELDS * TILES
GATHER_FROM, GATHER_SPAN = 24, 50
GATHER_FROM_FIRST = 30


def gather_pos(k, second=False):
    if second:
        return GATHER_FROM_FIRST + k * (GATHER_FROM + GATHER_SPAN - GATHER_FROM_FIRST) // GATHERS
    return GATHER_FROM + k * GATHER_SPAN // GATHERS


def last_user(q, ring):
    if q >= ring:
        return 0, q - ring
    return -1, max(x for x in range(NQ) if x % ring == q % ring)


def build(nc, ids, tables, w, dense, w1, b1, w2, b2, w3, ident, staircase, out):
    with ExitStack() as ctx:
        def sb(name, shape, dt=F32):
            return ctx.enter_context(nc.sbuf_tensor(name, shape, dt))

        def psum(name, shape):
            return ctx.enter_context(nc.psum_tensor(name, shape, F32))

        def sem(name):
            return ctx.enter_context(nc.semaphore(name))

        w_sb = sb("w_sb", [P, NB, P])
        stage = sb("stage", [P, 2, PART * P])
        ids_next = sb("ids_next", [P, TILES, FIELDS], I32)
        ids_now = sb("ids_now", [P, TILES, FIELDS], I32)
        raw = sb("raw", [P, TILES, FIELDS, EMB])
        hl = sb("hl", [P, 2, TILES, GROUP, 2, EMB])
        et = sb("et", [P, 2, 2, 2, CHUNK])
        v = sb("v", [P, GROUPS + 2, HI, CHUNK])
        prod = sb("prod", [P, PRODS, 2, HI, CHUNK])
        s_sb = sb("s_sb", [P, 2, 2, CHUNK])
        zt = sb("zt", [P, 2, 2, CHUNK])
        w1_sb = sb("w1_sb", [P, len(K_BLOCKS), H1])
        free = [w1_sb[:].rearrange("p k o -> p (k o)")[:, i * PART * P:(i + 1) * PART * P] for i in range(3)]
        w_hi, w_lo = free[:2], [stage[:, 0], stage[:, 1], free[2]]
        w2_sb = sb("w2_sb", [P, O1, H2])
        w3_sb = sb("w3_sb", [P, O2])
        b1_sb = sb("b1_sb", [P, O1])
        b2_sb = sb("b2_sb", [P, O2])
        h1_sb = sb("h1_sb", [P, O1, CHUNK])
        h2_sb = sb("h2_sb", [P, O2, CHUNK])
        y_sb = sb("y_sb", [1, CHUNK])
        id_sb = sb("id_sb", [P, P])
        stair = sb("stair", [P, 2 * P + GROUP])

        a_ps = psum("a_ps", [P, 2, 2, HI, CHUNK])
        z_ps = psum("z_ps", [P, 2, CHUNK])
        t_ps = psum("t_ps", [P, 2, CHUNK])
        h_ps = psum("h_ps", [P, O1, CHUNK])

        COPIES = 16 * 2 * QUARTERS
        const_in = sem("const_in")
        ids_in = sem("ids_in")
        top_in = sem("top_in")
        w_in = [sem(f"w_in{i}") for i in range(3)]
        hi_copied = [sem(f"hi_copied{i}") for i in range(2)]
        lo_copied = [sem(f"lo_copied{i}") for i in range(3)]
        ids_copied = sem("ids_copied")
        pool_passed = sem("pool_passed")
        gathered = [sem(f"gathered{g}") for g in range(GROUPS)]
        w_rounded = sem("w_rounded")
        w_split = sem("w_split")
        h_split = sem("h_split")
        l_split = sem("l_split")
        v_transposed = sem("v_transposed")
        e_transposed = sem("e_transposed")
        v_ready = sem("v_ready")
        e_ready = sem("e_ready")
        a_ready = sem("a_ready")
        multiplied = sem("multiplied")
        s_ready = sem("s_ready")
        summed = sem("summed")
        z_ready = sem("z_ready")
        dense_in = sem("dense_in")
        top1_done = sem("top1_done")
        h1_ready = sem("h1_ready")
        top2_done = sem("top2_done")
        h2_ready = sem("h2_ready")
        top3_done = sem("top3_done")
        y_ready = sem("y_ready")
        y_out = sem("y_out")
        y_free = sem("y_free")

        def chunks(eng, body, tail):
            body(0, True, False)
            with eng.Fori(1, CHUNKS - 1) as c:
                body(c, False, False)
            body(CHUNKS - 1, False, True)
            tail(CHUNKS)

        block = ctx.enter_context(nc.Block())

        @block.sync
        def _(sp):
            def ids_of(c):
                sp.dma_start(ids_next[:], ids[c]).then_inc(ids_in, 16)

            def w_of(p):
                sp.dma_start(w_lo[p % 3], w[p]).then_inc(w_in[p % 3], 16)

            def spread(p, of, to, copied):
                for quarter in range(QUARTERS):
                    at = p * PIECE + quarter * PART
                    n = min(PART, NB - at)
                    for copy in range(to, to + 2):
                        sp.dma_start(w_sb[EMB * copy:EMB * copy + EMB, at:at + n],
                                     of[EMB * quarter:EMB * quarter + EMB, 0:n * P]
                                     .rearrange("p (n c) -> p n c", c=P)).then_inc(copied, 16)

            ids_of(0)
            w_of(0)
            w_of(1)
            w_of(2)
            for p in range(PIECES):
                sp.wait_ge(w_rounded, p + 1)
                spread(p, w_hi[p % 2], 0, hi_copied[p % 2])
                sp.wait_ge(w_split, p + 1)
                spread(p, w_lo[p % 3], 2, lo_copied[p % 3])
                if 1 <= p < PIECES - 2:
                    sp.wait_ge(lo_copied[(p + 2) % 3], COPIES * ((p + 2) // 3))
                    w_of(p + 2)
            for p in range(PIECES - 3, PIECES):
                if p >= PIECES - 2:
                    sp.wait_ge(hi_copied[p % 2], COPIES * (p // 2 + 1))
                sp.wait_ge(lo_copied[p % 3], COPIES * (p // 3 + 1))
            sp.dma_start(w1_sb[:], w1).then_inc(top_in, 16)

            def dense_of(c):
                sp.wait_ge(top1_done, c * Z_TILES + Z_TILES - 2)
                sp.dma_start(zt[DENSE_ROW:ODD_ROW, (Z_TILES - 1) % 2, 0, :],
                             dense[:, bass.ds(c * CHUNK, CHUNK)]).then_inc(dense_in, 16)

            def result_of(c):
                sp.wait_ge(y_ready, c + 1)
                sp.dma_start(out[:, bass.ds(c * CHUNK, CHUNK)], y_sb[:]).then_inc(y_out, 16)
                sp.wait_ge(y_out, 16 * (c + 1))
                sp.sem_inc(y_free, 1)

            sp.sem_inc(y_free, 1)
            sp.wait_ge(ids_copied, 1)
            ids_of(1)
            dense_of(0)
            with sp.Fori(1, CHUNKS - 1) as c:
                sp.wait_ge(ids_copied, c + 1)
                sp.dma_start(ids_next[:],
                             ids[bass.ds(c + 1, 1)].rearrange("o p t f -> (o p) t f")).then_inc(ids_in, 16)
                result_of(c - 1)
                dense_of(c)
            result_of(CHUNKS - 2)
            dense_of(CHUNKS - 1)
            result_of(CHUNKS - 1)

        @block.gpsimd
        def _(pool):
            def waited():
                pool.sem_inc(pool_passed, 1)

            def take_ids(c, first):
                if not first:
                    for g in range(GROUPS):
                        pool.wait_ge(gathered[g], 16 * TILES * GROUP * c)
                pool.wait_ge(ids_in, 16 * (c + 1))
                waited()
                nc.gpsimd.tensor_copy(ids_now[:], ids_next[:]).then_inc(ids_copied, 1)
                pool.wait_ge(ids_copied, c + 1)
                waited()

            def gather(c, k, first):
                g, at = divmod(k, TILES * GROUP)
                t, f = at // GROUP, GROUP * g + at % GROUP
                if at == 0 and not first:
                    pool.wait_ge(l_split, GROUPS * (c - 1) + g + 1)
                    pool.wait_ge(v_transposed, GROUPS * (c - 1) + g + 1)
                    waited()
                pool.indirect_dma_start(
                    out=raw[:, t, f, :], out_offset=None, in_=tables[f],
                    in_offset=bass.IndirectOffsetOnAxis(ap=ids_now[:, t, f:f + 1], axis=0),
                ).then_inc(gathered[g], 16)

            def split_lo(c, g):
                pool.wait_ge(h_split, GROUPS * c + g + 1)
                waited()
                nc.gpsimd.tensor_tensor(
                    hl[:, g % 2, :, :, 1, :].bitcast(F32R), raw[:, :, GROUP * g:GROUP * g + GROUP, :],
                    hl[:, g % 2, :, :, 0, :], ALU.subtract).then_inc(l_split, 1)

            def body(c, second, end):
                if not end:
                    take_ids(c, False)
                for pos in range(GATHER_FROM, NQ if end else NQ + GATHER_FROM):
                    for ahead, g in splits_at(pos % NQ):
                        if not (ahead and end or second and pos < NQ and not ahead):
                            split_lo(c if ahead or pos >= NQ else c - 1, g)
                    for k in range(0 if end else GATHERS):
                        if gather_pos(k, second) == pos:
                            if second and k == 2:
                                split_lo(0, GROUPS - 1)
                            gather(c, k, False)

            take_ids(0, True)
            for k in range(GATHERS):
                gather(0, k, True)
                g, at = divmod(k, TILES * GROUP)
                if g and at == 2:
                    split_lo(0, g - 1)
            body(1, True, False)
            with pool.Fori(2, CHUNKS) as c:
                body(c, False, False)
            body(CHUNKS, False, True)

        @block.tensor
        def _(pe):
            mm = nc.tensor.matmul

            def transposes(c, kind, i, before, first):
                if not (first and before is None):
                    _, k, last = before or PREP[-1]
                    count = (c if before else c - 1) * (GROUPS if k == "V" else DOUBLES) + last + 1
                    pe.wait_ge(v_ready if k == "V" else e_ready, count)
                if kind == "V":
                    pe.wait_ge(gathered[i], 16 * TILES * GROUP * (c + 1))
                    for h in range(HI):
                        for t in range(TILES):
                            fields = raw[:, t, GROUP * i:GROUP * i + GROUP, :].rearrange("p f e -> p (f e)")
                            last = nc.tensor.transpose(
                                t_ps[:, h, P * t:P * t + P],
                                fields[:, h::HI], id_sb[:])
                    last.then_inc(v_transposed, 1)
                else:
                    g = 2 * i // HALF
                    pe.wait_ge(l_split, GROUPS * c + g + 1)
                    for n in range(2):
                        j = 2 * ORDER[2 * i + n] % GROUP
                        for t in range(TILES):
                            pair = hl[:, g % 2, t, j:j + 2].rearrange("p j s e -> p (j s e)")
                            last = nc.tensor.transpose(t_ps[:, n, P * t:P * t + P], pair, id_sb[:])
                    last.then_inc(e_transposed, 1)

            def a_of(c, q, first):
                n, half = QUADS[q][0], ODD[q]
                if not (first and q < 2):
                    pe.wait_ge(multiplied, NQ * c + q - 1)
                if n % 2 == 0 and q == START[n]:
                    pe.wait_ge(e_ready, DOUBLES * c + n // 2 + 1)
                if first:
                    p = BLOCK_AT[(q, 1, HI - 1)] // PIECE
                    if all(BLOCK_AT[(x, 1, HI - 1)] // PIECE < p for x in range(q)):
                        pe.wait_ge(hi_copied[p % 2], COPIES * (p // 2 + 1))
                        pe.wait_ge(lo_copied[p % 3], COPIES * (p // 3 + 1))
                for s in range(half, 2):
                    for h in range(HI):
                        last = mm(a_ps[:, q % 2, s, h, :],
                                  w_sb[:, BLOCK_AT[(q, s, h)], :].bitcast(F32R),
                                  et[:, n // 2 % 2, n % 2, s, :].bitcast(F32R), start=True, stop=True)
                last.then_inc(a_ready, 1)

            def sum_of(c, q, first):
                half = ODD[q]
                pe.wait_ge(s_ready, NQ * c + q + 1)
                k, row = Z_AT[q]
                if q == Z_START[k] and not (first and k == 0):
                    pe.wait_ge(z_ready, Z_TILES * c + k)
                mm(z_ps[:, half:2, :], stair[:, P - row:2 * P - row], s_sb[:, q % 2, half:2, :],
                   start=q == Z_START[k], stop=q + 1 == Z_END[k], skip_group_check=True).then_inc(summed, 1)

            def top1(c, k, unit, first):
                s, o = divmod(unit, O1)
                last_tile = k == Z_TILES - 1
                if unit == 0:
                    pe.wait_ge(z_ready, Z_TILES * c + k + 1)
                    if k == 0:
                        if first:
                            pe.wait_ge(top_in, 16 * 5)
                        else:
                            pe.wait_ge(y_ready, c)
                    if last_tile:
                        pe.wait_ge(dense_in, 16 * (c + 1))
                last = mm(h_ps[:, o, :], w1_sb[:, K_BLOCKS.index((k, s)), P * o:P * o + P], zt[:, k % 2, s, :],
                          start=k == 0 and s == 0 and o % 2 == 0, stop=last_tile, skip_group_check=True)
                if unit == (1 if last_tile else 2) * O1 - 1:
                    last.then_inc(top1_done, 1)

            def top2(c, unit):
                o, k = divmod(unit, O1)
                if unit == 0:
                    pe.wait_ge(h1_ready, O1 * (c + 1))
                last = mm(h_ps[:, o, :], w2_sb[:, k, P * o:P * o + P], h1_sb[:, k, :],
                          start=k == 0, stop=k == O1 - 1)
                if k == O1 - 1:
                    last.then_inc(top2_done, 1)

            def top3(c):
                pe.wait_ge(h2_ready, O2 * (c + 1))
                for k in range(O2):
                    last = mm(h_ps[0:1, 2, :], w3_sb[:, k:k + 1], h2_sb[:, k, :], start=k == 0, stop=k == O2 - 1)
                last.then_inc(top3_done, 1)

            def top1_at(c, pos, first, final=False):
                for k, at in enumerate(T1_AT_FINAL if final else T1_AT):
                    if pos in at:
                        top1(c, k, at.index(pos), first)

            def rest(c, pos, final=False):
                if pos < LAG:
                    sum_of(c - 1, NQ + pos - LAG, False)
                top1_at(c - 1, NQ + pos, False, final)
                if pos in T2_AT:
                    top2(c - 1, T2_AT.index(pos))
                if pos == T3_AT:
                    top3(c - 1)

            def body(c, first, final):
                if first:
                    for pos in range(-NQ, 0):
                        for _, kind, i, before in prep_at(pos, True):
                            transposes(0, kind, i, before, True)
                for pos in range(NQ):
                    a_of(c, pos, first)
                    for ahead, kind, i, before in prep_at(pos, first):
                        if not (ahead and final):
                            transposes(c + ahead, kind, i, before, False)
                    if not first:
                        rest(c, pos)
                    if pos >= LAG:
                        sum_of(c, pos - LAG, first)
                    top1_at(c, pos, first, final)

            def tail(c):
                for pos in range(T3_AT + 1):
                    rest(c, pos, True)

            pe.wait_ge(const_in, 32)
            chunks(pe, body, tail)

        @block.scalar
        def _(act):
            copy = nc.scalar.activation

            def round_pieces(pos):
                for p in pieces_at(pos):
                    act.wait_ge(w_in[p % 3], 16 * (p // 3 + 1))
                    if p >= 2:
                        act.wait_ge(w_split, p - 1)
                        act.wait_ge(hi_copied[p % 2], COPIES * (p // 2))
                    copy(w_hi[p % 2].bitcast(F32R), w_lo[p % 3], ACT.Copy).then_inc(w_rounded, 1)

            def split_hi(c, g, first):
                act.wait_ge(gathered[g], 16 * TILES * GROUP * (c + 1))
                if g >= 2:
                    act.wait_ge(e_transposed, DOUBLES * c + HALF // 2 * (g - 1))
                elif not first:
                    act.wait_ge(e_transposed, DOUBLES * c if g == 0 else DOUBLES * c - HALF // 2)
                copy(hl[:, g % 2, :, :, 0, :].bitcast(F32R), raw[:, :, GROUP * g:GROUP * g + GROUP, :],
                     ACT.Copy).then_inc(h_split, 1)

            def evacuate(c, kind, i, first):
                if kind == "V":
                    act.wait_ge(v_transposed, GROUPS * c + i + 1)
                    if not first:
                        act.wait_ge(multiplied, NQ * (c - 1) + last_use(i) + 1)
                    copies = [(slice(0, P), i, slice(0, P))]
                    if i < MIXED:
                        if i >= 2:
                            act.wait_ge(multiplied, NQ * c + last_use(MIX_B, G_START[2]) + 1)
                        if i % 2 == 0:
                            copies += [(slice(P // 2, P), MIX_A, slice(P // 2, P)), (slice(P // 2, P), MIX_B, slice(0, P // 2))]
                        else:
                            copies += [(slice(0, P // 2), MIX_A, slice(0, P // 2)), (slice(0, P // 2), MIX_B, slice(0, P // 2))]
                    for to, tile, of in copies:
                        last = copy(v[to, tile], t_ps[of], ACT.Copy)
                    last.then_inc(v_ready, 1)
                else:
                    act.wait_ge(e_transposed, DOUBLES * c + i + 1)
                    if i >= 2:
                        act.wait_ge(a_ready, NQ * c + END[2 * i - 3] + 1)
                    elif not first:
                        act.wait_ge(a_ready, NQ * (c - 1) + END[SOURCES + 2 * i - 3] + 1)
                    for s in range(2):
                        for half in range(2):
                            last = copy(et[64 * half:64 * half + 64, i % 2, :, s, :].bitcast(F32R),
                                        t_ps[64 * s:64 * s + 64], ACT.Copy)
                    last.then_inc(e_ready, 1)

            def z_of(c, k, first):
                act.wait_ge(summed, NQ * c + Z_END[k])
                if not (first and k < 2):
                    act.wait_ge(top1_done, Z_TILES * c + k - 1)
                if k < Z_TILES - 1:
                    copy(zt[:, k % 2], z_ps[:], ACT.Copy).then_inc(z_ready, 1)
                else:
                    copy(zt[0:DENSE_ROW, k % 2, 0], z_ps[0:DENSE_ROW, 0], ACT.Copy)
                    copy(zt[ODD_ROW:P, k % 2, 0], z_ps[0:P - ODD_ROW, 1], ACT.Copy).then_inc(z_ready, 1)

            def rest(c, pos):
                if pos == LAG - 1:
                    z_of(c - 1, Z_TILES - 1, False)
                if pos == H1_AT:
                    act.wait_ge(top1_done, Z_TILES * c)
                    for o in range(O1):
                        copy(h1_sb[:, o, :], h_ps[:, o, :], ACT.Relu, bias=b1_sb[:, o:o + 1]).then_inc(h1_ready, 1)
                if pos == H2_AT:
                    act.wait_ge(top2_done, O2 * c)
                    for o in range(O2):
                        copy(h2_sb[:, o, :], h_ps[:, o, :], ACT.Relu, bias=b2_sb[:, o:o + 1]).then_inc(h2_ready, 1)
                if pos == T3_AT:
                    act.wait_ge(top3_done, c)
                    result(c)

            def result(c):
                act.wait_ge(y_free, c)
                copy(y_sb[:], h_ps[0:1, 2, :], ACT.Copy).then_inc(y_ready, 1)

            def body(c, first, final):
                if first:
                    round_pieces(-1)
                    split_hi(0, 0, True)
                    for pos in range(-NQ, 0):
                        for _, kind, i, _ in prep_at(pos, True):
                            evacuate(0, kind, i, True)
                for pos in range(NQ):
                    if first:
                        round_pieces(pos)
                    for ahead, g in splits_at(pos):
                        if not (ahead and final):
                            split_hi(c + ahead, g, first and not ahead)
                    if not first:
                        rest(c, pos)
                    for ahead, kind, i, _ in prep_at(pos, first):
                        if not (ahead and final):
                            evacuate(c + ahead, kind, i, first and not ahead)
                    for k in range(Z_TILES - 1):
                        if pos == Z_END[k] - 1 + LAG:
                            z_of(c, k, first)

            def tail(c):
                for pos in range(T3_AT + 1):
                    rest(c, pos)

            act.dma_start(id_sb[:], ident).then_inc(const_in, 16)
            act.dma_start(stair[:], staircase).then_inc(const_in, 16)
            act.dma_start(b1_sb[:], b1).then_inc(top_in, 16)
            act.dma_start(b2_sb[:], b2).then_inc(top_in, 16)
            act.dma_start(w3_sb[:], w3).then_inc(top_in, 16)
            act.dma_start(w2_sb[:], w2).then_inc(top_in, 16)
            chunks(act, body, tail)

        @block.vector
        def _(dve):
            tt = nc.vector.tensor_tensor

            def split_pieces(pos):
                for p in pieces_at(pos):
                    dve.wait_ge(w_rounded, p + 1)
                    tt(w_lo[p % 3].bitcast(F32R), w_lo[p % 3], w_hi[p % 2], ALU.subtract).then_inc(w_split, 1)

            def multiply(c, q, first):
                t, half = QUADS[q][2], ODD[q]
                back, user = last_user(q, PRODS)
                if not (first and back):
                    dve.wait_ge(s_ready, NQ * (c + back) + user + 1)
                dve.wait_ge(a_ready, NQ * c + q + 1)
                if all(NEEDS[x] < NEEDS[q] for x in range(q)):
                    dve.wait_ge(v_ready, GROUPS * c + NEEDS[q] + 1)
                k = 2 - half
                tt(prod[:, q % PRODS, half:2].rearrange("p s h b -> p s (h b)"),
                   a_ps[:, q % 2, half:2].rearrange("p s h b -> p s (h b)"),
                   v[:, t].rearrange("p h b -> p (h b)").unsqueeze(1).broadcast_to([P, k, HI * CHUNK]),
                   ALU.mult).then_inc(multiplied, 1)

            def add(c, q, first):
                half = ODD[q]
                dve.wait_ge(multiplied, NQ * c + q + 1)
                if not (first and q < 2):
                    dve.wait_ge(summed, NQ * c + q - 1)
                tt(s_sb[:, q % 2, half:2], prod[:, q % PRODS, half:2, 0, :], prod[:, q % PRODS, half:2, 1, :],
                   ALU.add).then_inc(s_ready, 1)

            def body(c, first, final):
                if first:
                    split_pieces(-1)
                for pos in range(NQ):
                    if first:
                        split_pieces(pos)
                    multiply(c, pos, first)
                    if pos:
                        add(c, pos - 1, first)
                    elif not first:
                        add(c - 1, NQ - 1, False)

            def tail(c):
                add(c - 1, NQ - 1, False)

            chunks(dve, body, tail)


def kernel(**inputs):
    import numpy as np
    import concourse.bacc as bacc
    from concourse.bass_utils import run_bass_kernel_spmd

    nc = bacc.Bacc("TRN2", target_bir_lowering=False, num_devices=1)
    arrays = {}

    def given(name, a):
        arrays[name] = np.ascontiguousarray(a)
        return nc.dram_tensor(name, a.shape, mybir.dt.from_np(a.dtype), kind="ExternalInput").ap()

    i_of, j_of = np.triu_indices(FIELDS, k=1)
    pair = -np.ones((FIELDS, FIELDS), np.int64)
    pair[i_of, j_of] = np.arange(len(i_of))

    ids = np.asarray(inputs["ids"]).reshape(CHUNKS, TILES, P, FIELDS).transpose(0, 2, 1, 3)

    w_in = np.asarray(inputs["L0_rec_W"])
    w = np.zeros((EMB, PIECES * PIECE, GROUP, LO), w_in.dtype)
    w1_in = np.asarray(inputs["W_top1"])
    w1 = np.zeros((P, len(K_BLOCKS), H1), w1_in.dtype)
    for q, (_, _, _, slots) in enumerate(QUADS):
        for (u, s), (i, j) in slots.items():
            k = pair[min(i, j), max(i, j)]
            both = w_in[k] if j < i else w_in[k].T
            for h in range(HI):
                w[:, BLOCK_AT[q, s, h], u, :] = both[:, h::HI]
            tile, row = Z_AT[q]
            if tile < Z_TILES - 1:
                w1[row + u, K_BLOCKS.index((tile, s))] = w1_in[k]
            else:
                w1[row + u + ODD_ROW * s, -1] = w1_in[k]
    w1[DENSE_ROW:ODD_ROW, -1] = w1_in[len(i_of):]

    stair = np.zeros((P, 2 * P + GROUP), np.float32)
    stair[np.arange(P), P + np.arange(P) // LO] = 1

    args = [
        given("ids_d", ids),
        [given(f"tbl_{f}_d", np.asarray(inputs[f"tbl_{f}"])) for f in range(FIELDS)],
        given("w_d", w.reshape(EMB, PIECES, QUARTERS, -1).transpose(1, 2, 0, 3).reshape(PIECES, P, -1)),
        given("dense_d", np.asarray(inputs["dense_ctx"]).T),
        given("w_top1_d", w1),
        given("b_top1_d", np.asarray(inputs["b_top1"]).reshape(O1, P).T),
        given("w_top2_d", np.asarray(inputs["W_top2"]).reshape(O1, P, H2).transpose(1, 0, 2)),
        given("b_top2_d", np.asarray(inputs["b_top2"]).reshape(O2, P).T),
        given("w_top3_d", np.asarray(inputs["W_top3"]).reshape(O2, P).T),
        given("ident_d", np.eye(P, dtype=np.float32)),
        given("stair_d", stair),
    ]
    y = nc.dram_tensor("y_d", (1, BATCH), F32, kind="ExternalOutput").ap()
    build(nc, *args, y)
    r = run_bass_kernel_spmd(nc, [arrays], core_ids=[0])
    return r.results[0]["y_d"].reshape(BATCH, 1)
```

```python
from contextlib import ExitStack

import concourse.bass as bass
from concourse import mybir

F32 = mybir.dt.float32
F32R = mybir.dt.float32r
I32 = mybir.dt.int32
ALU = mybir.AluOpType
ACT = mybir.ActivationFunctionType

P = 128
BATCH, FIELDS, EMB = 2048, 40, 32
DENSE = 16
H1, H2 = 512, 256
CHUNK = 256
TILES = CHUNK // P
CHUNKS = BATCH // CHUNK
GROUP = 8
GROUPS = FIELDS // GROUP
LO = P // GROUP
HI = EMB // LO
SOURCES = FIELDS // 2

HALF = GROUP // 2
MIX_A, MIX_B = GROUPS, GROUPS + 1
MIXED = 4


def tile_fields(tile, double):
    if tile < GROUPS:
        return [GROUP * tile + u for u in range(GROUP)]
    first = 2 * GROUP * double
    low = first + (HALF if tile == MIX_A else 0)
    return [first + GROUP + u for u in range(HALF)] + [low + u for u in range(HALF)]


def plan():
    order, quads, met = [], [], set()
    work = []
    for g in range(GROUPS):
        ms = [HALF * g + u for u in range(HALF)]
        if g < MIXED:
            tiles = [[g], [MIX_A]] if g % 2 == 0 else [[MIX_B], [g - 1, g]]
            low, high = ms[:2], ms[2:]
            work += [(m, tiles[0]) for m in low]
            work += [(m, tiles[1]) for m in high[::-1]]
        else:
            work += [(m, [g]) for m in ms]
    for m, own in work:
        double = m // GROUP
        before = list(range(2 * double)) if HALF * MIXED > m else list(range(MIXED))
        for tile in before + own:
            slots = {}
            for s in (1, 0):
                for u, i in enumerate(tile_fields(tile, double)):
                    j = 2 * m + s
                    if i != j and frozenset((i, j)) not in met:
                        met.add(frozenset((i, j)))
                        slots[u, s] = i, j
            quads.append((len(order), m, tile, slots))
        order.append(m)
    assert len(met) == FIELDS * (FIELDS - 1) // 2
    return order, quads


ORDER, QUADS = plan()
NQ = len(QUADS)
ODD = [int(all(s for _, s in x[3])) for x in QUADS]
START = [min(q for q, x in enumerate(QUADS) if x[0] == n) for n in range(SOURCES)]
END = [max(q for q, x in enumerate(QUADS) if x[0] == n) for n in range(SOURCES)]
G_START = [START[HALF * g] for g in range(GROUPS)]


def last_use(tile, before=NQ):
    return max((q for q in range(before) if QUADS[q][2] == tile), default=None)


NEEDS = [tile if tile < GROUPS else m // GROUP * 2 + 1 for _, m, tile, _ in QUADS]


BLOCKS = [(q, s, h) for q in range(NQ) for s in range(ODD[q], 2) for h in range(HI)]
BLOCK_AT = {b: n for n, b in enumerate(BLOCKS)}
NB = len(BLOCKS)
PART = 8
QUARTERS = P // EMB
PIECE = QUARTERS * PART
PIECES = -(-NB // PIECE)
HI_RING, LO_RING = 2, 3
PIECE_POS = [-1, -1, 0, 2, 4, 8, 12]


def rows_of_z():
    at, tile, row = [], 0, 0
    for _, _, _, slots in QUADS:
        low, high = min(u for u, _ in slots), max(u for u, _ in slots) + 1
        if row + high - low > P:
            tile, row = tile + 1, 0
        at.append((tile, row - low))
        row += high - low
    return at, row


Z_AT, LAST_ROWS = rows_of_z()
Z_TILES = Z_AT[-1][0] + 1
Z_START = [min(q for q in range(NQ) if Z_AT[q][0] == k) for k in range(Z_TILES)]
Z_END = [max(q for q in range(NQ) if Z_AT[q][0] == k) + 1 for k in range(Z_TILES)]
ODD_ROW = P // 2
DENSE_ROW = ODD_ROW - DENSE
assert LAST_ROWS <= DENSE_ROW
K_BLOCKS = [(k, s) for k in range(Z_TILES - 1) for s in range(2)] + [(Z_TILES - 1, 0)]
O1, O2 = H1 // P, H2 // P

LAG = 5
PAIRS = NQ // 2
RING = 4
assert NQ % RING == 0
T1_AT = [[38, 39, 40, 41, 43, 44, 45, 46], [47, 49, 51, 53, 55, 57, 58, 59],
         [NQ + p for p in (5, 7, 8, 10, 12, 13, 14, 16)], [NQ + p for p in (17, 19, 20, 21)]]
T1_AT_FINAL = [[38, 39, 40, 41, 42, 43, 44, 45], [46, 47, 48, 49, 50, 51, 52, 53],
               [56, 57, 58, 58, 59, 61, 61, 61], [62, 62, 62, 62]]
H1_AT, T2_AT, H2_AT, T3_AT = 22, [25, 26, 27, 28, 29, 30, 31, 33], 34, 36
assert NQ % 2 == 0 and SOURCES % 4 == 0 and Z_TILES == 4
assert all(at[0] > end + LAG for at, end in zip(T1_AT, Z_END))
assert all(at[0] >= end + LAG for at, end in zip(T1_AT_FINAL, Z_END))
assert T1_AT[3][-1] < NQ + H1_AT < NQ + T2_AT[0] and T2_AT[-1] < H2_AT < T3_AT < T1_AT[0][0] - 1
assert T1_AT[0][-1] < Z_END[2] + LAG and T1_AT[2][-1] < NQ + Z_END[0] + LAG
assert T1_AT[1][-1] < Z_END[3] + LAG and T1_AT[3][-1] < NQ + Z_END[1] + LAG


V_POS, E_POS = [-4, -2, 9, 15, 33], [-8, -6, 0, 2, 6, 11, 18, 24, 31, 42]
V_POS_FIRST, E_POS_FIRST = [-4, 1, 9, 15, 33], [-8, -6, 2, 3, 7, 11, 18, 24, 31, 42]
DOUBLES = SOURCES // 2
ET_SLOT = [1, 2, 0, 1, 2, 1, 0, 1, 2, 0]


def field_prep(v_pos, e_pos):
    prep = [(p, "V", g) for g, p in enumerate(v_pos)] + [(p, "E", d) for d, p in enumerate(e_pos)]
    return sorted(prep, key=lambda x: x[0])


def last_double(d):
    before = [x for x in range(d) if ET_SLOT[x] == ET_SLOT[d]]
    return (0, before[-1]) if before else (-1, max(x for x in range(DOUBLES) if ET_SLOT[x] == ET_SLOT[d]))


SPLIT_POS = [-11, -4, 2, 12, 26]
SPLIT_POS_FIRST = [None, 0, 5, 14, 28]
PREP = field_prep(V_POS, E_POS)
PREP_FIRST = field_prep(V_POS_FIRST, E_POS_FIRST)
assert PREP[-1] == PREP_FIRST[-1]


def prep_at(pos, first):
    for place, (p, kind, i) in enumerate(PREP_FIRST if first else PREP):
        if p == pos:
            yield 0, kind, i, ((PREP_FIRST if first else PREP)[place - 1] if place else None)
    for place, (p, kind, i) in enumerate(PREP):
        if p + NQ == pos:
            yield 1, kind, i, (PREP[place - 1] if place else None)


def splits_at(pos, first=False):
    for g in range(GROUPS):
        if (SPLIT_POS_FIRST if first else SPLIT_POS)[g] == pos:
            yield 0, g
        if SPLIT_POS[g] + NQ == pos:
            yield 1, g


def pieces_at(pos):
    return [p for p in range(PIECES) if PIECE_POS[p] == pos]


assert all(PIECE_POS[BLOCK_AT[q, 1, HI - 1] // PIECE] <= q for q in range(NQ))


GATHERS = FIELDS * TILES
GATHER_FROM, GATHER_SPAN = 24, 50
GATHER_FROM_FIRST = 30


def gather_pos(k, second=False):
    if second:
        return GATHER_FROM_FIRST + k * (GATHER_FROM + GATHER_SPAN - GATHER_FROM_FIRST) // GATHERS
    return GATHER_FROM + k * GATHER_SPAN // GATHERS


def build(nc, ids, tables, w, dense, w1, b1, w2, b2, w3, ident, staircase, out):
    with ExitStack() as ctx:
        def sb(name, shape, dt=F32):
            return ctx.enter_context(nc.sbuf_tensor(name, shape, dt))

        def psum(name, shape):
            return ctx.enter_context(nc.psum_tensor(name, shape, F32))

        def sem(name):
            return ctx.enter_context(nc.semaphore(name))

        w_sb = sb("w_sb", [P, NB, P])
        ids_next = sb("ids_next", [P, TILES, FIELDS], I32)
        ids_now = sb("ids_now", [P, TILES, FIELDS], I32)
        raw = sb("raw", [P, TILES, FIELDS, EMB])
        hl = sb("hl", [P, 2, TILES, GROUP, 2, EMB])
        et = sb("et", [P, 3, 2, 2, CHUNK])
        v = sb("v", [P, GROUPS + 2, HI, CHUNK])
        prod = sb("prod", [P, RING, 2, HI, CHUNK])
        s_sb = sb("s_sb", [P, RING, 2, CHUNK])
        zt = sb("zt", [P, 2, 2, CHUNK])
        w1_sb = sb("w1_sb", [P, len(K_BLOCKS), H1])
        w2_sb = sb("w2_sb", [P, O1, H2])
        w3_sb = sb("w3_sb", [P, O2])
        b1_sb = sb("b1_sb", [P, O1])
        b2_sb = sb("b2_sb", [P, O2])
        h1_sb = sb("h1_sb", [P, O1, CHUNK])
        h2_sb, y_sb = h1_sb[:, 0:O2], h1_sb[0:1, O2]
        assert O1 * CHUNK == PART * P == O1 * H2
        id_sb = sb("id_sb", [P, P])
        stair = sb("stair", [P, 2 * P + GROUP])

        free = [w1_sb[:].rearrange("p k o -> p (k o)")[:, i * PART * P:(i + 1) * PART * P] for i in range(3)]
        w_hi = free[:HI_RING]
        w_lo = [w2_sb[:].rearrange("p k o -> p (k o)"), h1_sb[:].rearrange("p o b -> p (o b)"), free[HI_RING]]
        assert len(w_lo) == LO_RING

        a_ps = psum("a_ps", [P, 2, 2, HI, CHUNK])
        z_ps = psum("z_ps", [P, 2, CHUNK])
        t_ps = psum("t_ps", [P, 2, CHUNK])
        h_ps = psum("h_ps", [P, O1, CHUNK])

        COPIES = 16 * 2 * QUARTERS
        const_in = sem("const_in")
        ids_in = sem("ids_in")
        top_in = sem("top_in")
        w_in = [sem(f"w_in{i}") for i in range(LO_RING)]
        hi_copied = [sem(f"hi_copied{i}") for i in range(HI_RING)]
        lo_copied = [sem(f"lo_copied{i}") for i in range(LO_RING)]
        ids_copied = sem("ids_copied")
        pool_passed = sem("pool_passed")
        gathered = [sem(f"gathered{g}") for g in range(GROUPS)]
        w_rounded = sem("w_rounded")
        w_split = sem("w_split")
        h_split = sem("h_split")
        l_split = sem("l_split")
        v_transposed = sem("v_transposed")
        e_transposed = sem("e_transposed")
        v_ready = sem("v_ready")
        e_ready = sem("e_ready")
        a_ready = sem("a_ready")
        multiplied = sem("multiplied")
        s_ready = sem("s_ready")
        summed = sem("summed")
        z_ready = sem("z_ready")
        dense_in = sem("dense_in")
        top1_done = sem("top1_done")
        h1_ready = sem("h1_ready")
        top2_done = sem("top2_done")
        h2_ready = sem("h2_ready")
        top3_done = sem("top3_done")
        y_ready = sem("y_ready")
        y_out = sem("y_out")
        y_free = sem("y_free")

        def lo_of(eng, g):
            eng.tensor_tensor(hl[:, g % 2, :, :, 1, :].bitcast(F32R), raw[:, :, GROUP * g:GROUP * g + GROUP, :],
                              hl[:, g % 2, :, :, 0, :], ALU.subtract).then_inc(l_split, 1)

        def chunks(eng, body, tail):
            body(0, True, False)
            with eng.Fori(1, CHUNKS - 1) as c:
                body(c, False, False)
            body(CHUNKS - 1, False, True)
            tail(CHUNKS)

        block = ctx.enter_context(nc.Block())

        @block.sync
        def _(sp):
            def ids_of(c):
                sp.dma_start(ids_next[:], ids[c]).then_inc(ids_in, 16)

            def w_of(p):
                sp.dma_start(w_lo[p % LO_RING], w[p]).then_inc(w_in[p % LO_RING], 16)

            def spread(p, of, to, copied):
                for quarter in range(QUARTERS):
                    at = p * PIECE + quarter * PART
                    n = min(PART, NB - at)
                    for copy in (to, to + 1):
                        sp.dma_start(w_sb[EMB * copy:EMB * copy + EMB, at:at + n],
                                     of[EMB * quarter:EMB * quarter + EMB, 0:n * P]
                                     .rearrange("p (n c) -> p n c", c=P)).then_inc(copied, 16)

            ids_of(0)
            w_of(0)
            w_of(1)
            w_of(2)
            for p in range(PIECES):
                sp.wait_ge(w_rounded, p + 1)
                spread(p, w_hi[p % HI_RING], 0, hi_copied[p % HI_RING])
                sp.wait_ge(w_split, p + 1)
                spread(p, w_lo[p % LO_RING], 2, lo_copied[p % LO_RING])
                ahead = p + LO_RING - 1
                if LO_RING <= ahead < PIECES:
                    sp.wait_ge(lo_copied[ahead % LO_RING], COPIES * (ahead // LO_RING))
                    w_of(ahead)
            for p in range(PIECES - LO_RING, PIECES):
                if p >= PIECES - HI_RING:
                    sp.wait_ge(hi_copied[p % HI_RING], COPIES * (p // HI_RING + 1))
                sp.wait_ge(lo_copied[p % LO_RING], COPIES * (p // LO_RING + 1))
            sp.dma_start(w1_sb[:], w1).then_inc(top_in, 16)
            sp.dma_start(w2_sb[:], w2).then_inc(top_in, 16)

            def dense_of(c):
                sp.wait_ge(top1_done, c * Z_TILES + Z_TILES - 2)
                sp.dma_start(zt[DENSE_ROW:ODD_ROW, (Z_TILES - 1) % 2, 0, :],
                             dense[:, bass.ds(c * CHUNK, CHUNK)]).then_inc(dense_in, 16)

            def result_of(c):
                sp.wait_ge(y_ready, c + 1)
                sp.dma_start(out[:, bass.ds(c * CHUNK, CHUNK)], y_sb).then_inc(y_out, 16)
                sp.wait_ge(y_out, 16 * (c + 1))
                sp.sem_inc(y_free, 1)

            sp.sem_inc(y_free, 1)
            sp.wait_ge(ids_copied, 1)
            ids_of(1)
            dense_of(0)
            with sp.Fori(1, CHUNKS - 1) as c:
                sp.wait_ge(ids_copied, c + 1)
                sp.dma_start(ids_next[:],
                             ids[bass.ds(c + 1, 1)].rearrange("o p t f -> (o p) t f")).then_inc(ids_in, 16)
                result_of(c - 1)
                dense_of(c)
            result_of(CHUNKS - 2)
            dense_of(CHUNKS - 1)
            result_of(CHUNKS - 1)

        @block.gpsimd
        def _(pool):
            def waited():
                pool.sem_inc(pool_passed, 1)

            def take_ids(c, first):
                if not first:
                    for g in range(GROUPS):
                        pool.wait_ge(gathered[g], 16 * TILES * GROUP * c)
                pool.wait_ge(ids_in, 16 * (c + 1))
                waited()
                nc.gpsimd.tensor_copy(ids_now[:], ids_next[:]).then_inc(ids_copied, 1)
                pool.wait_ge(ids_copied, c + 1)
                waited()

            def gather(c, k, first):
                g, at = divmod(k, TILES * GROUP)
                t, f = at // GROUP, GROUP * g + at % GROUP
                if at == 0 and not first:
                    pool.wait_ge(l_split, GROUPS * (c - 1) + g + 1)
                    pool.wait_ge(v_transposed, GROUPS * (c - 1) + g + 1)
                    waited()
                pool.indirect_dma_start(
                    out=raw[:, t, f, :], out_offset=None, in_=tables[f],
                    in_offset=bass.IndirectOffsetOnAxis(ap=ids_now[:, t, f:f + 1], axis=0),
                ).then_inc(gathered[g], 16)

            def split_lo(c, g):
                pool.wait_ge(h_split, GROUPS * c + g + 1)
                if g == 0:
                    pool.wait_ge(l_split, GROUPS * c)
                waited()
                lo_of(nc.gpsimd, g)

            def body(c, second, end):
                if not end:
                    take_ids(c, False)
                for pos in range(GATHER_FROM, NQ if end else NQ + GATHER_FROM):
                    for ahead, g in splits_at(pos % NQ):
                        if not (ahead and end or second and pos < NQ and not ahead):
                            split_lo(c if ahead or pos >= NQ else c - 1, g)
                    for k in range(0 if end else GATHERS):
                        if gather_pos(k, second) == pos:
                            gather(c, k, False)

            take_ids(0, True)
            for k in range(GATHERS):
                gather(0, k, True)
            body(1, True, False)
            with pool.Fori(2, CHUNKS) as c:
                body(c, False, False)
            body(CHUNKS, False, True)

        @block.tensor
        def _(pe):
            mm = nc.tensor.matmul

            def transposes(c, kind, i, before, first):
                if not (first and before is None):
                    _, k, last = before or PREP[-1]
                    count = (c if before else c - 1) * (GROUPS if k == "V" else DOUBLES) + last + 1
                    pe.wait_ge(v_ready if k == "V" else e_ready, count)
                if kind == "V":
                    pe.wait_ge(gathered[i], 16 * TILES * GROUP * (c + 1))
                    for h in range(HI):
                        for t in range(TILES):
                            fields = raw[:, t, GROUP * i:GROUP * i + GROUP, :].rearrange("p f e -> p (f e)")
                            last = nc.tensor.transpose(
                                t_ps[:, h, P * t:P * t + P],
                                fields[:, h::HI], id_sb[:])
                    last.then_inc(v_transposed, 1)
                else:
                    g = 2 * i // HALF
                    pe.wait_ge(l_split, GROUPS * c + g + 1)
                    for n in range(2):
                        j = 2 * ORDER[2 * i + n] % GROUP
                        for t in range(TILES):
                            pair = hl[:, g % 2, t, j:j + 2].rearrange("p j s e -> p (j s e)")
                            last = nc.tensor.transpose(t_ps[:, n, P * t:P * t + P], pair, id_sb[:])
                    last.then_inc(e_transposed, 1)

            def a_of(c, q, first):
                n, half = QUADS[q][0], ODD[q]
                if not (first and q < 2):
                    pe.wait_ge(multiplied, NQ * c + q - 1)
                if n % 2 == 0 and q == START[n]:
                    pe.wait_ge(e_ready, DOUBLES * c + n // 2 + 1)
                if first:
                    p = BLOCK_AT[(q, 1, HI - 1)] // PIECE
                    if all(BLOCK_AT[(x, 1, HI - 1)] // PIECE < p for x in range(q)):
                        pe.wait_ge(hi_copied[p % HI_RING], COPIES * (p // HI_RING + 1))
                        pe.wait_ge(lo_copied[p % LO_RING], COPIES * (p // LO_RING + 1))
                for s in range(half, 2):
                    for h in range(HI):
                        last = mm(a_ps[:, q % 2, s, h, :],
                                  w_sb[:, BLOCK_AT[(q, s, h)], :].bitcast(F32R),
                                  et[:, ET_SLOT[n // 2], n % 2, s, :].bitcast(F32R), start=True, stop=True)
                last.then_inc(a_ready, 1)

            def sum_of(c, q, first):
                half = ODD[q]
                pe.wait_ge(s_ready, PAIRS * c + q // 2 + 1)
                k, row = Z_AT[q]
                if q == Z_START[k] and not (first and k == 0):
                    pe.wait_ge(z_ready, Z_TILES * c + k)
                mm(z_ps[:, half:2, :], stair[:, P - row:2 * P - row], s_sb[:, q % RING, half:2, :],
                   start=q == Z_START[k], stop=q + 1 == Z_END[k], skip_group_check=True).then_inc(summed, 1)

            def top1(c, k, unit, first):
                s, o = divmod(unit, O1)
                last_tile = k == Z_TILES - 1
                if unit == 0:
                    pe.wait_ge(z_ready, Z_TILES * c + k + 1)
                    if k == 0:
                        if first:
                            pe.wait_ge(top_in, 16 * 5)
                        else:
                            pe.wait_ge(y_ready, c)
                    if last_tile:
                        pe.wait_ge(dense_in, 16 * (c + 1))
                last = mm(h_ps[:, o, :], w1_sb[:, K_BLOCKS.index((k, s)), P * o:P * o + P], zt[:, k % 2, s, :],
                          start=k == 0 and s == 0 and o % 2 == 0, stop=last_tile, skip_group_check=True)
                if unit == (1 if last_tile else 2) * O1 - 1:
                    last.then_inc(top1_done, 1)

            def top2(c, unit):
                o, k = divmod(unit, O1)
                if o == 0 and k != 1:
                    pe.wait_ge(h1_ready, O1 * c + max(k, 1) + 1)
                last = mm(h_ps[:, o, :], w2_sb[:, k, P * o:P * o + P], h1_sb[:, k, :],
                          start=k == 0, stop=k == O1 - 1)
                if k == O1 - 1:
                    last.then_inc(top2_done, 1)

            def top3(c):
                pe.wait_ge(h2_ready, O2 * (c + 1))
                for k in range(O2):
                    last = mm(h_ps[0:1, 2, :], w3_sb[:, k:k + 1], h2_sb[:, k, :], start=k == 0, stop=k == O2 - 1)
                last.then_inc(top3_done, 1)

            def top1_at(c, pos, first, final=False):
                for k, at in enumerate(T1_AT_FINAL if final else T1_AT):
                    for unit in range(len(at)):
                        if at[unit] == pos:
                            top1(c, k, unit, first)

            def rest(c, pos, final=False):
                if pos < LAG:
                    sum_of(c - 1, NQ + pos - LAG, False)
                top1_at(c - 1, NQ + pos, False, final)
                if pos in T2_AT:
                    top2(c - 1, T2_AT.index(pos))
                if pos == T3_AT:
                    top3(c - 1)

            def body(c, first, final):
                if first:
                    for pos in range(-NQ, 0):
                        for _, kind, i, before in prep_at(pos, True):
                            transposes(0, kind, i, before, True)
                for pos in range(NQ):
                    a_of(c, pos, first)
                    for ahead, kind, i, before in prep_at(pos, first):
                        if not (ahead and final):
                            transposes(c + ahead, kind, i, before, False)
                    if not first:
                        rest(c, pos)
                    if pos >= LAG:
                        sum_of(c, pos - LAG, first)
                    top1_at(c, pos, first, final)

            def tail(c):
                for pos in range(T3_AT + 1):
                    rest(c, pos, True)

            pe.wait_ge(const_in, 32)
            chunks(pe, body, tail)

        @block.scalar
        def _(act):
            copy = nc.scalar.activation

            def round_pieces(pos):
                for p in pieces_at(pos):
                    act.wait_ge(w_in[p % LO_RING], 16 * (p // LO_RING + 1))
                    if p >= HI_RING:
                        act.wait_ge(w_split, p - HI_RING + 1)
                        act.wait_ge(hi_copied[p % HI_RING], COPIES * (p // HI_RING))
                    copy(w_hi[p % HI_RING].bitcast(F32R), w_lo[p % LO_RING], ACT.Copy).then_inc(w_rounded, 1)

            def split_hi(c, g, first):
                act.wait_ge(gathered[g], 16 * TILES * GROUP * (c + 1))
                if g >= 2:
                    act.wait_ge(e_transposed, DOUBLES * c + HALF // 2 * (g - 1))
                elif not first:
                    act.wait_ge(e_transposed, DOUBLES * c if g == 0 else DOUBLES * c - HALF // 2)
                copy(hl[:, g % 2, :, :, 0, :].bitcast(F32R), raw[:, :, GROUP * g:GROUP * g + GROUP, :],
                     ACT.Copy).then_inc(h_split, 1)

            def evacuate(c, kind, i, first):
                if kind == "V":
                    act.wait_ge(v_transposed, GROUPS * c + i + 1)
                    if not first:
                        act.wait_ge(multiplied, NQ * (c - 1) + last_use(i) + 1)
                    copies = [(slice(0, P), i, slice(0, P))]
                    if i < MIXED:
                        if i >= 2:
                            act.wait_ge(multiplied, NQ * c + last_use(MIX_B, G_START[2]) + 1)
                        lower, upper = slice(0, P // 2), slice(P // 2, P)
                        if i % 2 == 0:
                            copies += [(upper, MIX_A, upper), (upper, MIX_B, lower)]
                        else:
                            copies += [(lower, MIX_A, lower), (lower, MIX_B, lower)]
                    for to, tile, of in copies:
                        last = copy(v[to, tile], t_ps[of], ACT.Copy)
                    last.then_inc(v_ready, 1)
                else:
                    act.wait_ge(e_transposed, DOUBLES * c + i + 1)
                    back, user = last_double(i)
                    if not (first and back):
                        act.wait_ge(a_ready, NQ * (c + back) + END[2 * user + 1] + 1)
                    for s in range(2):
                        for half in range(2):
                            last = copy(et[64 * half:64 * half + 64, ET_SLOT[i], :, s, :].bitcast(F32R),
                                        t_ps[64 * s:64 * s + 64], ACT.Copy)
                    last.then_inc(e_ready, 1)

            def z_of(c, k, first):
                act.wait_ge(summed, NQ * c + Z_END[k])
                if not (first and k < 2):
                    act.wait_ge(top1_done, Z_TILES * c + k - 1)
                if k < Z_TILES - 1:
                    copy(zt[:, k % 2], z_ps[:], ACT.Copy).then_inc(z_ready, 1)
                else:
                    copy(zt[0:DENSE_ROW, k % 2, 0], z_ps[0:DENSE_ROW, 0], ACT.Copy)
                    copy(zt[ODD_ROW:P, k % 2, 0], z_ps[0:P - ODD_ROW, 1], ACT.Copy).then_inc(z_ready, 1)

            def rest(c, pos):
                if pos == LAG - 1:
                    z_of(c - 1, Z_TILES - 1, False)
                if pos == H1_AT:
                    act.wait_ge(top1_done, Z_TILES * c)
                    act.wait_ge(y_free, c)
                    for o in range(O1):
                        copy(h1_sb[:, o, :], h_ps[:, o, :], ACT.Relu, bias=b1_sb[:, o:o + 1]).then_inc(h1_ready, 1)
                if pos == H2_AT:
                    act.wait_ge(top2_done, O2 * c)
                    for o in range(O2):
                        copy(h2_sb[:, o, :], h_ps[:, o, :], ACT.Relu, bias=b2_sb[:, o:o + 1]).then_inc(h2_ready, 1)
                if pos == T3_AT:
                    act.wait_ge(top3_done, c)
                    result(c)

            def result(c):
                copy(y_sb, h_ps[0:1, 2, :], ACT.Copy).then_inc(y_ready, 1)

            def body(c, first, final):
                if first:
                    round_pieces(-1)
                    split_hi(0, 0, True)
                    for pos in range(-NQ, 0):
                        for _, kind, i, _ in prep_at(pos, True):
                            evacuate(0, kind, i, True)
                for pos in range(NQ):
                    if first:
                        round_pieces(pos)
                    for ahead, g in splits_at(pos, first):
                        if not (ahead and final):
                            split_hi(c + ahead, g, first and not ahead)
                    if not first:
                        rest(c, pos)
                    for ahead, kind, i, _ in prep_at(pos, first):
                        if not (ahead and final):
                            evacuate(c + ahead, kind, i, first and not ahead)
                    for k in range(Z_TILES - 1):
                        if pos == Z_END[k] - 1 + LAG:
                            z_of(c, k, first)

            def tail(c):
                for pos in range(T3_AT + 1):
                    rest(c, pos)

            act.dma_start(id_sb[:], ident).then_inc(const_in, 16)
            act.dma_start(stair[:], staircase).then_inc(const_in, 16)
            act.dma_start(b1_sb[:], b1).then_inc(top_in, 16)
            act.dma_start(b2_sb[:], b2).then_inc(top_in, 16)
            act.dma_start(w3_sb[:], w3).then_inc(top_in, 16)
            chunks(act, body, tail)

        @block.vector
        def _(dve):
            tt = nc.vector.tensor_tensor

            def split_pieces(pos):
                for p in pieces_at(pos):
                    dve.wait_ge(w_rounded, p + 1)
                    lo = w_lo[p % LO_RING]
                    tt(lo.bitcast(F32R), lo, w_hi[p % HI_RING], ALU.subtract).then_inc(w_split, 1)

            def multiply(c, q, first):
                t, half = QUADS[q][2], ODD[q]
                if not (first and q < RING):
                    dve.wait_ge(s_ready, PAIRS * c + (q - RING) // 2 + 1)
                dve.wait_ge(a_ready, NQ * c + q + 1)
                if all(NEEDS[x] < NEEDS[q] for x in range(q)):
                    dve.wait_ge(v_ready, GROUPS * c + NEEDS[q] + 1)
                k = 2 - half
                tt(prod[:, q % RING, half:2].rearrange("p s h b -> p s (h b)"),
                   a_ps[:, q % 2, half:2].rearrange("p s h b -> p s (h b)"),
                   v[:, t].rearrange("p h b -> p (h b)").unsqueeze(1).broadcast_to([P, k, HI * CHUNK]),
                   ALU.mult).then_inc(multiplied, 1)

            def add(c, k, first):
                dve.wait_ge(multiplied, NQ * c + 2 * k + 2)
                if not (first and 2 * k < RING):
                    dve.wait_ge(summed, NQ * c + 2 * k + 2 - RING)
                ring = slice(2 * k % RING, 2 * k % RING + 2)
                tt(s_sb[:, ring], prod[:, ring, :, 0, :], prod[:, ring, :, 1, :], ALU.add).then_inc(s_ready, 1)

            def body(c, first, final):
                if first:
                    split_pieces(-1)
                    dve.wait_ge(h_split, 1)
                    lo_of(nc.vector, 0)
                for pos in range(NQ):
                    if first:
                        split_pieces(pos)
                        for ahead, g in splits_at(pos - 1, True):
                            if not ahead:
                                dve.wait_ge(h_split, g + 1)
                                lo_of(nc.vector, g)
                    multiply(c, pos, first)
                    if pos and pos % 2 == 0:
                        add(c, pos // 2 - 1, first)
                    elif pos == 0 and not first:
                        add(c - 1, PAIRS - 1, False)

            def tail(c):
                add(c - 1, PAIRS - 1, False)

            chunks(dve, body, tail)


def kernel(**inputs):
    import numpy as np
    import concourse.bacc as bacc
    from concourse.bass_utils import run_bass_kernel_spmd

    nc = bacc.Bacc("TRN2", target_bir_lowering=False, num_devices=1)
    arrays = {}

    def given(name, a):
        arrays[name] = np.ascontiguousarray(a)
        return nc.dram_tensor(name, a.shape, mybir.dt.from_np(a.dtype), kind="ExternalInput").ap()

    i_of, j_of = np.triu_indices(FIELDS, k=1)
    pair = -np.ones((FIELDS, FIELDS), np.int64)
    pair[i_of, j_of] = np.arange(len(i_of))

    ids = np.asarray(inputs["ids"]).reshape(CHUNKS, TILES, P, FIELDS).transpose(0, 2, 1, 3)

    w_in = np.asarray(inputs["L0_rec_W"])
    w = np.zeros((EMB, PIECES * PIECE, GROUP, LO), w_in.dtype)
    w1_in = np.asarray(inputs["W_top1"])
    w1 = np.zeros((P, len(K_BLOCKS), H1), w1_in.dtype)
    for q, (_, _, _, slots) in enumerate(QUADS):
        for (u, s), (i, j) in slots.items():
            k = pair[min(i, j), max(i, j)]
            both = w_in[k] if j < i else w_in[k].T
            for h in range(HI):
                w[:, BLOCK_AT[q, s, h], u, :] = both[:, h::HI]
            tile, row = Z_AT[q]
            if tile < Z_TILES - 1:
                w1[row + u, K_BLOCKS.index((tile, s))] = w1_in[k]
            else:
                w1[row + u + ODD_ROW * s, -1] = w1_in[k]
    w1[DENSE_ROW:ODD_ROW, -1] = w1_in[len(i_of):]

    stair = np.zeros((P, 2 * P + GROUP), np.float32)
    stair[np.arange(P), P + np.arange(P) // LO] = 1

    args = [
        given("ids_d", ids),
        [given(f"tbl_{f}_d", np.asarray(inputs[f"tbl_{f}"])) for f in range(FIELDS)],
        given("w_d", w.reshape(EMB, PIECES, QUARTERS, -1).transpose(1, 2, 0, 3).reshape(PIECES, P, -1)),
        given("dense_d", np.asarray(inputs["dense_ctx"]).T),
        given("w_top1_d", w1),
        given("b_top1_d", np.asarray(inputs["b_top1"]).reshape(O1, P).T),
        given("w_top2_d", np.asarray(inputs["W_top2"]).reshape(O1, P, H2).transpose(1, 0, 2)),
        given("b_top2_d", np.asarray(inputs["b_top2"]).reshape(O2, P).T),
        given("w_top3_d", np.asarray(inputs["W_top3"]).reshape(O2, P).T),
        given("ident_d", np.eye(P, dtype=np.float32)),
        given("stair_d", stair),
    ]
    y = nc.dram_tensor("y_d", (1, BATCH), F32, kind="ExternalOutput").ap()
    build(nc, *args, y)
    r = run_bass_kernel_spmd(nc, [arrays], core_ids=[0])
    return r.results[0]["y_d"].reshape(BATCH, 1)
```
